# Optimizing a Trainium2 kernel written in Bass

```python
import numpy as np
import jax
import jax.numpy as jnp

def _softmax(x, axis=-1):
    return jax.nn.softmax(x, axis=axis)

def _gelu(x):
    return jax.nn.gelu(x, approximate=True)

def _silu(x):
    return jax.nn.silu(x)

def _sigmoid(x):
    return jax.nn.sigmoid(x)

def _layernorm(x, axis=-1, eps=1e-05):
    m = jnp.mean(x, axis=axis, keepdims=True)
    v = jnp.var(x, axis=axis, keepdims=True)
    return (x - m) / jnp.sqrt(v + eps)

def _scatter_add(tgt, idx, src, axis=0):
    return tgt.at[idx].add(src)

def _segment_sum(src, seg, n):
    return jax.ops.segment_sum(src, seg, n)
kernel_name = 'mk_seq_postln_d2_jaxref_r8_bca8c4'

def setup_inputs(seed: int=0):
    np.random.seed(seed)
    _w = jnp.asarray

    def _L0_attn_setup():
        import jax, jax.numpy as jnp
        import numpy as np
        D_MODEL = 256
        D_STATE = 64
        EXPAND = 2
        N_HEADS = 64
        NGROUPS = 1
        MIMO_RANK = 1
        D_INNER = EXPAND * D_MODEL
        HEAD_DIM = D_INNER // N_HEADS
        HEADS_PER_GROUP = N_HEADS // NGROUPS
        SSD_SCALE = (D_STATE * MIMO_RANK) ** (-0.5)
        EPS = 1e-06
        BATCH, SEQ = (2, 256)

        def _rms(v):
            return v * jax.lax.rsqrt(jnp.mean(v * v, axis=-1, keepdims=True) + EPS)

        def _rope(v, phi):
            v1, v2 = (v[..., 0::2], v[..., 1::2])
            c, s = (jnp.cos(phi), jnp.sin(phi))
            r1 = v1 * c - v2 * s
            r2 = v1 * s + v2 * c
            return jnp.stack([r1, r2], axis=-1).reshape(v.shape)
        key = jax.random.key(seed)
        ks = jax.random.split(key, 10)
        d_in_proj = 2 * D_INNER + 2 * NGROUPS * MIMO_RANK * D_STATE + N_HEADS
        return {'x': jax.random.normal(ks[0], (BATCH, SEQ, D_MODEL), jnp.float32), 'W_in': jax.random.normal(ks[1], (D_MODEL, d_in_proj), jnp.float32) * 0.02, 'W_out': jax.random.normal(ks[2], (D_INNER, D_MODEL), jnp.float32) * 0.02, 'dt_bias': jax.random.normal(ks[3], (N_HEADS,), jnp.float32) * 0.1, 'A_log': jnp.log(jax.random.uniform(ks[4], (N_HEADS,), jnp.float32, 1.0, 16.0)), 'D_param': jnp.ones((N_HEADS,), jnp.float32), 'B_bias': jax.random.normal(ks[5], (N_HEADS, D_STATE), jnp.float32) * 0.02, 'C_bias': jax.random.normal(ks[6], (N_HEADS, D_STATE), jnp.float32) * 0.02, 'rope_freqs': jax.random.uniform(ks[7], (N_HEADS, D_STATE // 2), jnp.float32, 0.0, 1.0), 'norm_w': jnp.ones((D_INNER,), jnp.float32)}
    _L0_attn_in = _L0_attn_setup()

    def _L0_ffn_setup():
        import jax, jax.numpy as jnp
        import numpy as np
        TOP_K = 2
        SCALING = 2.0
        key = jax.random.key(seed)
        ks = jax.random.split(key, 10)
        B, S, H, I, E, R = (1, 64, 256, 128, 8, 16)
        w = 1.0 / np.sqrt(H)
        inp = {'x': jax.random.normal(ks[0], (B, S, H), jnp.float32), 'gate_weight': jax.random.normal(ks[1], (E, H), jnp.float32) * w, 'gate_lora_A': jax.random.normal(ks[2], (R, H), jnp.float32) * 0.02, 'gate_lora_B': jax.random.normal(ks[3], (E, R), jnp.float32) * 0.02, 'gate_up_proj': jax.random.normal(ks[4], (E, H, 2 * I), jnp.float32) * w, 'down_proj': jax.random.normal(ks[5], (E, I, H), jnp.float32) * (1.0 / np.sqrt(I)), 'gup_lora_A': jax.random.normal(ks[6], (E, R, H), jnp.float32) * 0.02, 'gup_lora_B': jax.random.normal(ks[7], (E, 2 * I, R), jnp.float32) * 0.02, 'down_lora_A': jax.random.normal(ks[8], (E, R, I), jnp.float32) * 0.02, 'down_lora_B': jax.random.normal(ks[9], (E, H, R), jnp.float32) * 0.02}
        return inp
    _L0_ffn_in = _L0_ffn_setup()

    def _L1_attn_setup():
        import jax, jax.numpy as jnp
        import numpy as np
        B, S, DIM = (1, 256, 256)
        HEADS, KV_HEADS = (32, 8)
        DH = DIM // HEADS
        G = HEADS // KV_HEADS
        CBLK = 16
        SBLK = 16
        NSEL = 8
        WIN = 64
        SCALE = DH ** (-0.5)
        NEG = -1e+30
        CDIM = CBLK * DH

        def _rope(x, pos):
            d = x.shape[-1]
            inv = 1.0 / 10000.0 ** (jnp.arange(0, d, 2, dtype=jnp.float32) / d)
            ang = pos[:, None] * inv[None, :]
            cos, sin = (jnp.cos(ang), jnp.sin(ang))
            x1, x2 = (x[..., 0::2], x[..., 1::2])
            return jnp.stack([x1 * cos - x2 * sin, x1 * sin + x2 * cos], axis=-1).reshape(x.shape)

        def _forward(x, w_qkv, k_pos, v_pos, k_cw1, k_cb1, k_cw2, k_cb2, v_cw1, v_cb1, v_cw2, v_cb2, mem_ck, mem_cv, w_gate, b_gate, w_out):
            b, n, _ = x.shape
            di, dkv = (HEADS * DH, KV_HEADS * DH)
            qkv = x @ w_qkv
            q = qkv[..., :di].reshape(b, n, KV_HEADS, G, DH).transpose(0, 2, 3, 1, 4)
            k = qkv[..., di:di + dkv].reshape(b, n, KV_HEADS, DH).transpose(0, 2, 1, 3)
            v = qkv[..., di + dkv:].reshape(b, n, KV_HEADS, DH).transpose(0, 2, 1, 3)
            nc = n // CBLK
            kb = k[:, :, :nc * CBLK].reshape(b, KV_HEADS, nc, CBLK, DH) + k_pos[None, :, None]
            vb = v[:, :, :nc * CBLK].reshape(b, KV_HEADS, nc, CBLK, DH) + v_pos[None, :, None]
            ck = jax.nn.relu(kb.reshape(b, KV_HEADS, nc, CDIM) @ k_cw1 + k_cb1) @ k_cw2 + k_cb2
            cv = jax.nn.relu(vb.reshape(b, KV_HEADS, nc, CDIM) @ v_cw1 + v_cb1) @ v_cw2 + v_cb2
            ck = jnp.concatenate([jnp.broadcast_to(mem_ck[None], (b, KV_HEADS, 1, DH)), ck], axis=2)
            cv = jnp.concatenate([jnp.broadcast_to(mem_cv[None], (b, KV_HEADS, 1, DH)), cv], axis=2)
            csim = jnp.einsum('bhgnd,bhjd->bhgnj', q, ck) * SCALE
            ck_last = jnp.concatenate([jnp.array([-1]), (jnp.arange(nc) + 1) * CBLK - 1])
            cmask = ck_last[None, :] < jnp.arange(n)[:, None]
            csim = jnp.where(cmask, csim, NEG)
            c_out = jnp.einsum('bhgnj,bhjd->bhgnd', jax.nn.softmax(csim, -1), cv)
            imp = csim[..., 1:].mean(axis=2)
            imp = jnp.concatenate([jnp.full(imp.shape[:-1] + (1,), -1000.0, imp.dtype), imp], axis=-1)
            imp = jax.nn.softmax(imp, -1)[..., 1:]
            sel_vals, sel_idx = jax.lax.top_k(imp, NSEL)
            fine_gate_mask = sel_vals > 1e-10
            pos = jnp.arange(n, dtype=jnp.float32)
            rq, rk = (_rope(q, pos), _rope(k, pos))
            nf = n // SBLK
            own = jnp.broadcast_to((jnp.arange(n) // SBLK)[None, None, :, None], (b, KV_HEADS, n, 1))
            idx = jnp.concatenate([sel_idx, own], axis=-1)
            kblocks = rk.reshape(b, KV_HEADS, nf, SBLK, DH)
            vblocks = v.reshape(b, KV_HEADS, nf, SBLK, DH)
            bi = jnp.arange(b)[:, None, None, None]
            hi = jnp.arange(KV_HEADS)[None, :, None, None]
            fk = kblocks[bi, hi, idx].reshape(b, KV_HEADS, n, (NSEL + 1) * SBLK, DH)
            fv = vblocks[bi, hi, idx].reshape(b, KV_HEADS, n, (NSEL + 1) * SBLK, DH)
            sel_m = jnp.repeat(fine_gate_mask[..., None], SBLK, -1).reshape(b, KV_HEADS, n, NSEL * SBLK)
            diag_m = (jnp.arange(n) % SBLK)[:, None] >= jnp.arange(SBLK)[None, :]
            fmask = jnp.concatenate([sel_m, jnp.broadcast_to(diag_m[None, None], (b, KV_HEADS, n, SBLK))], axis=-1)
            fsim = jnp.einsum('bhgnd,bhnjd->bhgnj', rq, fk) * SCALE
            fsim = jnp.where(fmask[:, :, None], fsim, NEG)
            f_out = jnp.einsum('bhgnj,bhnjd->bhgnd', jax.nn.softmax(fsim, -1), fv)
            nwin = n // WIN
            qw = rq.reshape(b, KV_HEADS, G, nwin, WIN, DH)
            kw = rk.reshape(b, KV_HEADS, nwin, WIN, DH)
            vw = v.reshape(b, KV_HEADS, nwin, WIN, DH)
            kcat = jnp.concatenate([jnp.concatenate([jnp.zeros_like(kw[:, :, :1]), kw[:, :, :-1]], 2), kw], 3)
            vcat = jnp.concatenate([jnp.concatenate([jnp.zeros_like(vw[:, :, :1]), vw[:, :, :-1]], 2), vw], 3)
            ssim = jnp.einsum('bhgwid,bhwjd->bhgwij', qw, kcat) * SCALE
            i_, j_ = (jnp.arange(WIN), jnp.arange(2 * WIN))
            delta = i_[:, None] - (j_[None, :] - WIN)
            smask = ((delta >= 0) & (delta <= WIN))[None] & ((jnp.arange(nwin) > 0)[:, None, None] | (j_ >= WIN)[None, None, :])
            ssim = jnp.where(smask[None, None, None], ssim, NEG)
            s_out = jnp.einsum('bhgwij,bhwjd->bhgwid', jax.nn.softmax(ssim, -1), vcat)
            s_out = s_out.reshape(b, KV_HEADS, G, n, DH)
            gates = jax.nn.sigmoid(x @ w_gate + b_gate).reshape(b, n, KV_HEADS, G, 3).transpose(0, 2, 3, 1, 4)
            out = gates[..., 0:1] * c_out + gates[..., 1:2] * f_out + gates[..., 2:3] * s_out
            out = out.transpose(0, 3, 1, 2, 4).reshape(b, n, HEADS * DH)
            return out @ w_out
        key = jax.random.key(seed)
        ks = jax.random.split(key, 16)

        def rnd(i, shape, sc=0.02):
            return jax.random.normal(ks[i], shape, dtype=jnp.float32) * sc
        dim_inner, dim_kv = (HEADS * DH, KV_HEADS * DH)
        return {'hidden_states': jax.random.normal(ks[0], (B, S, DIM), dtype=jnp.float32), 'w_qkv': rnd(1, (DIM, dim_inner + 2 * dim_kv)), 'k_pos': rnd(2, (KV_HEADS, CBLK, DH)), 'v_pos': rnd(3, (KV_HEADS, CBLK, DH)), 'k_cw1': rnd(4, (CDIM, CDIM)), 'k_cb1': jnp.zeros((CDIM,), jnp.float32), 'k_cw2': rnd(5, (CDIM, DH)), 'k_cb2': jnp.zeros((DH,), jnp.float32), 'v_cw1': rnd(6, (CDIM, CDIM)), 'v_cb1': jnp.zeros((CDIM,), jnp.float32), 'v_cw2': rnd(7, (CDIM, DH)), 'v_cb2': jnp.zeros((DH,), jnp.float32), 'mem_ck': rnd(8, (KV_HEADS, 1, DH)), 'mem_cv': rnd(9, (KV_HEADS, 1, DH)), 'w_gate': rnd(10, (DIM, 3 * HEADS)), 'b_gate': jnp.tile(jnp.array([-2.0, -2.0, 2.0], jnp.float32), HEADS), 'w_out': rnd(11, (dim_inner, DIM))}
    _L1_attn_in = _L1_attn_setup()

    def _L1_ffn_setup():
        import jax, jax.numpy as jnp
        import numpy as np
        B, S, H = (4, 128, 256)
        NH = 16
        HD = H // NH
        RD = HD // 2
        LAT = H // 4
        I = 128
        NE = 8
        NSH = 1
        NR = NE - NSH
        TOPK = 2
        EPS = 1e-05
        SCALING = 8.0

        def _w(key, shape, fan_in):
            return jax.random.normal(key, shape, dtype=jnp.float32) / np.sqrt(fan_in)

        def rmsnorm(x, w):
            rms = jax.lax.rsqrt(jnp.mean(x * x, axis=-1, keepdims=True) + EPS)
            return w * rms * x

        def rope_cos_sin(seq_len):
            inv_freq = 1.0 / 10000.0 ** (jnp.arange(0, RD, 2, dtype=jnp.float32) / RD)
            t = jnp.arange(seq_len, dtype=jnp.float32)
            ang = jnp.outer(t, inv_freq)
            emb = jnp.concatenate([ang, ang], axis=-1)
            return (jnp.cos(emb), jnp.sin(emb))

        def apply_rope(x, cos, sin):
            c = cos[None, :, None, :]
            s = sin[None, :, None, :]
            x1, x2 = jnp.split(x, 2, axis=-1)
            rot = jnp.concatenate([-x2, x1], axis=-1)
            return x * c + rot * s

        def expert_ffn(x, wg, wu, wd):
            h = jax.nn.silu(x @ wg) * (x @ wu) / SCALING
            return h @ wd

        def attention(x, kv_d_w, q_d_w, k_u_w, v_u_w, q_u_w, rope_k_w, rope_q_w, o_w):
            b, s, _ = x.shape
            kv_d = x @ kv_d_w
            q_d = x @ q_d_w
            k_p = (kv_d @ k_u_w).reshape(b, s, NH, RD)
            q_p = (q_d @ q_u_w).reshape(b, s, NH, RD)
            v = (kv_d @ v_u_w).reshape(b, s, NH, HD)
            k_r = (x @ rope_k_w).reshape(b, s, NH, RD)
            q_r = (q_d @ rope_q_w).reshape(b, s, NH, RD)
            cos, sin = rope_cos_sin(s)
            k_r = apply_rope(k_r, cos, sin)
            q_r = apply_rope(q_r, cos, sin)
            k = jnp.concatenate([k_p, k_r], axis=-1)
            q = jnp.concatenate([q_p, q_r], axis=-1)
            scale = 1.0 / np.sqrt(HD)
            scores = jnp.einsum('bqhd,bkhd->bhqk', q, k) * scale
            causal = jnp.tril(jnp.ones((s, s), dtype=bool))
            scores = jnp.where(causal[None, None], scores, jnp.finfo(scores.dtype).min)
            probs = jax.nn.softmax(scores, axis=-1)
            out = jnp.einsum('bhqk,bkhd->bqhd', probs, v).reshape(b, s, H)
            return out @ o_w

        def moe(x, sh_gate, sh_up, sh_down, r_gate, r_up, r_down, router_w, router_b):
            shared = expert_ffn(x, sh_gate, sh_up, sh_down)
            logits = x @ router_w + router_b
            probs = jax.nn.sigmoid(logits)
            scores, idx = jax.lax.top_k(probs, TOPK)
            scores = scores / jnp.sum(scores, axis=-1, keepdims=True)
            w = jnp.sum(jax.nn.one_hot(idx, NR, dtype=x.dtype) * scores[..., None], axis=-2)
            combined = jnp.zeros_like(x)
            for e in range(NR):
                combined = combined + w[..., e:e + 1] * expert_ffn(x, r_gate[e], r_up[e], r_down[e])
            return shared + combined
        key = jax.random.key(seed)
        ks = jax.random.split(key, 24)
        return {'x': jax.random.normal(ks[0], (B, S, H), dtype=jnp.float32), 'ln1_w': jnp.ones((H,), jnp.float32), 'ln2_w': jnp.ones((H,), jnp.float32), 'kv_d_w': _w(ks[1], (H, LAT), H), 'q_d_w': _w(ks[2], (H, LAT), H), 'k_u_w': _w(ks[3], (LAT, H // 2), LAT), 'v_u_w': _w(ks[4], (LAT, H), LAT), 'q_u_w': _w(ks[5], (LAT, H // 2), LAT), 'rope_k_w': _w(ks[6], (H, H // 2), H), 'rope_q_w': _w(ks[7], (LAT, H // 2), LAT), 'o_w': _w(ks[8], (H, H), H), 'sh_gate': _w(ks[9], (H, I), H), 'sh_up': _w(ks[10], (H, I), H), 'sh_down': _w(ks[11], (I, H), I), 'r_gate': _w(ks[12], (NR, H, I), H), 'r_up': _w(ks[13], (NR, H, I), H), 'r_down': _w(ks[14], (NR, I, H), I), 'router_w': _w(ks[15], (H, NR), H), 'router_b': jnp.zeros((NR,), jnp.float32)}
    _L1_ffn_in = _L1_ffn_setup()
    _d = {'L0_attn_x': _L0_attn_in['x'], 'L0_attn_W_in': _L0_attn_in['W_in'], 'L0_attn_W_out': _L0_attn_in['W_out'], 'L0_attn_dt_bias': _L0_attn_in['dt_bias'], 'L0_attn_A_log': _L0_attn_in['A_log'], 'L0_attn_D_param': _L0_attn_in['D_param'], 'L0_attn_B_bias': _L0_attn_in['B_bias'], 'L0_attn_C_bias': _L0_attn_in['C_bias'], 'L0_attn_rope_freqs': _L0_attn_in['rope_freqs'], 'L0_attn_norm_w': _L0_attn_in['norm_w'], 'L0_ffn_gate_weight': _L0_ffn_in['gate_weight'], 'L0_ffn_gate_lora_A': _L0_ffn_in['gate_lora_A'], 'L0_ffn_gate_lora_B': _L0_ffn_in['gate_lora_B'], 'L0_ffn_gate_up_proj': _L0_ffn_in['gate_up_proj'], 'L0_ffn_down_proj': _L0_ffn_in['down_proj'], 'L0_ffn_gup_lora_A': _L0_ffn_in['gup_lora_A'], 'L0_ffn_gup_lora_B': _L0_ffn_in['gup_lora_B'], 'L0_ffn_down_lora_A': _L0_ffn_in['down_lora_A'], 'L0_ffn_down_lora_B': _L0_ffn_in['down_lora_B'], 'L1_attn_w_qkv': _L1_attn_in['w_qkv'], 'L1_attn_k_pos': _L1_attn_in['k_pos'], 'L1_attn_v_pos': _L1_attn_in['v_pos'], 'L1_attn_k_cw1': _L1_attn_in['k_cw1'], 'L1_attn_k_cb1': _L1_attn_in['k_cb1'], 'L1_attn_k_cw2': _L1_attn_in['k_cw2'], 'L1_attn_k_cb2': _L1_attn_in['k_cb2'], 'L1_attn_v_cw1': _L1_attn_in['v_cw1'], 'L1_attn_v_cb1': _L1_attn_in['v_cb1'], 'L1_attn_v_cw2': _L1_attn_in['v_cw2'], 'L1_attn_v_cb2': _L1_attn_in['v_cb2'], 'L1_attn_mem_ck': _L1_attn_in['mem_ck'], 'L1_attn_mem_cv': _L1_attn_in['mem_cv'], 'L1_attn_w_gate': _L1_attn_in['w_gate'], 'L1_attn_b_gate': _L1_attn_in['b_gate'], 'L1_attn_w_out': _L1_attn_in['w_out'], 'L1_ffn_ln1_w': _L1_ffn_in['ln1_w'], 'L1_ffn_ln2_w': _L1_ffn_in['ln2_w'], 'L1_ffn_kv_d_w': _L1_ffn_in['kv_d_w'], 'L1_ffn_q_d_w': _L1_ffn_in['q_d_w'], 'L1_ffn_k_u_w': _L1_ffn_in['k_u_w'], 'L1_ffn_v_u_w': _L1_ffn_in['v_u_w'], 'L1_ffn_q_u_w': _L1_ffn_in['q_u_w'], 'L1_ffn_rope_k_w': _L1_ffn_in['rope_k_w'], 'L1_ffn_rope_q_w': _L1_ffn_in['rope_q_w'], 'L1_ffn_o_w': _L1_ffn_in['o_w'], 'L1_ffn_sh_gate': _L1_ffn_in['sh_gate'], 'L1_ffn_sh_up': _L1_ffn_in['sh_up'], 'L1_ffn_sh_down': _L1_ffn_in['sh_down'], 'L1_ffn_r_gate': _L1_ffn_in['r_gate'], 'L1_ffn_r_up': _L1_ffn_in['r_up'], 'L1_ffn_r_down': _L1_ffn_in['r_down'], 'L1_ffn_router_w': _L1_ffn_in['router_w'], 'L1_ffn_router_b': _L1_ffn_in['router_b']}
    _x0 = _d['L0_attn_x']
    _d['L0_attn_x'] = jax.random.normal(jax.random.fold_in(jax.random.key(seed), 1), (4, 1024, 256), dtype=_x0.dtype)
    del _x0
    return _d

def reference(L0_attn_x, L0_attn_W_in, L0_attn_W_out, L0_attn_dt_bias, L0_attn_A_log, L0_attn_D_param, L0_attn_B_bias, L0_attn_C_bias, L0_attn_rope_freqs, L0_attn_norm_w, L0_ffn_gate_weight, L0_ffn_gate_lora_A, L0_ffn_gate_lora_B, L0_ffn_gate_up_proj, L0_ffn_down_proj, L0_ffn_gup_lora_A, L0_ffn_gup_lora_B, L0_ffn_down_lora_A, L0_ffn_down_lora_B, L1_attn_w_qkv, L1_attn_k_pos, L1_attn_v_pos, L1_attn_k_cw1, L1_attn_k_cb1, L1_attn_k_cw2, L1_attn_k_cb2, L1_attn_v_cw1, L1_attn_v_cb1, L1_attn_v_cw2, L1_attn_v_cb2, L1_attn_mem_ck, L1_attn_mem_cv, L1_attn_w_gate, L1_attn_b_gate, L1_attn_w_out, L1_ffn_ln1_w, L1_ffn_ln2_w, L1_ffn_kv_d_w, L1_ffn_q_d_w, L1_ffn_k_u_w, L1_ffn_v_u_w, L1_ffn_q_u_w, L1_ffn_rope_k_w, L1_ffn_rope_q_w, L1_ffn_o_w, L1_ffn_sh_gate, L1_ffn_sh_up, L1_ffn_sh_down, L1_ffn_r_gate, L1_ffn_r_up, L1_ffn_r_down, L1_ffn_router_w, L1_ffn_router_b):

    def _L0_attn_ref(x, W_in, W_out, dt_bias, A_log, D_param, B_bias, C_bias, rope_freqs, norm_w):
        import jax, jax.numpy as jnp
        import numpy as np
        D_MODEL = 256
        D_STATE = 64
        EXPAND = 2
        N_HEADS = 64
        NGROUPS = 1
        MIMO_RANK = 1
        D_INNER = EXPAND * D_MODEL
        HEAD_DIM = D_INNER // N_HEADS
        HEADS_PER_GROUP = N_HEADS // NGROUPS
        SSD_SCALE = (D_STATE * MIMO_RANK) ** (-0.5)
        EPS = 1e-06
        BATCH, SEQ = (2, 256)

        def _rms(v):
            return v * jax.lax.rsqrt(jnp.mean(v * v, axis=-1, keepdims=True) + EPS)

        def _rope(v, phi):
            v1, v2 = (v[..., 0::2], v[..., 1::2])
            c, s = (jnp.cos(phi), jnp.sin(phi))
            r1 = v1 * c - v2 * s
            r2 = v1 * s + v2 * c
            return jnp.stack([r1, r2], axis=-1).reshape(v.shape)
        Bsz, T, _ = x.shape
        zxbcdt = x @ W_in
        z = zxbcdt[..., :D_INNER]
        xs = zxbcdt[..., D_INNER:2 * D_INNER]
        o = 2 * D_INNER
        gn = NGROUPS * D_STATE
        Braw = zxbcdt[..., o:o + gn].reshape(Bsz, T, NGROUPS, D_STATE)
        Craw = zxbcdt[..., o + gn:o + 2 * gn].reshape(Bsz, T, NGROUPS, D_STATE)
        dt_raw = zxbcdt[..., o + 2 * gn:]
        dt = jax.nn.softplus(dt_raw + dt_bias)
        a = jnp.exp(-jnp.exp(A_log) * dt)
        Bh = jnp.repeat(_rms(Braw), HEADS_PER_GROUP, axis=2) + B_bias
        Ch = jnp.repeat(_rms(Craw), HEADS_PER_GROUP, axis=2) + C_bias
        phi = jnp.cumsum(dt, axis=1)[..., None] * rope_freqs
        Bh = _rope(Bh, phi)
        Ch = _rope(Ch, phi)
        xh = xs.reshape(Bsz, T, N_HEADS, HEAD_DIM)
        u = xh * dt[..., None]

        def step(h, inp):
            a_t, u_t, b_t, c_t = inp
            h = a_t[..., None, None] * h + u_t[..., None] * b_t[:, :, None, :]
            y = jnp.einsum('bhpn,bhn->bhp', h, c_t)
            return (h, y)
        h0 = jnp.zeros((Bsz, N_HEADS, HEAD_DIM, D_STATE), x.dtype)
        xs_time = (a.transpose(1, 0, 2), u.transpose(1, 0, 2, 3), Bh.transpose(1, 0, 2, 3), Ch.transpose(1, 0, 2, 3))
        _, ys = jax.lax.scan(step, h0, xs_time)
        ys = ys.transpose(1, 0, 2, 3)
        y = SSD_SCALE * ys + D_param[None, None, :, None] * xh
        y = y.reshape(Bsz, T, D_INNER)
        g = y * jax.nn.silu(z)
        y = g * jax.lax.rsqrt(jnp.mean(g * g, axis=-1, keepdims=True) + EPS) * norm_w
        return y @ W_out

    def _L0_ffn_ref(x, gate_weight, gate_lora_A, gate_lora_B, gate_up_proj, down_proj, gup_lora_A, gup_lora_B, down_lora_A, down_lora_B):
        import jax, jax.numpy as jnp
        import numpy as np
        TOP_K = 2
        SCALING = 2.0
        B, S, H = x.shape
        xf = x.reshape(-1, H)
        gate_delta = SCALING * (gate_lora_B @ gate_lora_A)
        router_logits = xf @ gate_weight.T + xf @ gate_delta.T
        probs = jax.nn.softmax(router_logits.astype(jnp.float32), axis=-1)
        routing_weights, selected = jax.lax.top_k(probs, TOP_K)
        routing_weights = routing_weights / routing_weights.sum(-1, keepdims=True)
        routing_weights = routing_weights.astype(xf.dtype)
        gup = jnp.einsum('th,eho->teo', xf, gate_up_proj)
        gup = gup + SCALING * jnp.einsum('ter,eor->teo', jnp.einsum('th,erh->ter', xf, gup_lora_A), gup_lora_B)
        gates, h = jnp.split(gup, 2, axis=-1)
        h = jax.nn.silu(gates) * h
        out = jnp.einsum('tei,eih->teh', h, down_proj)
        out = out + SCALING * jnp.einsum('ter,ehr->teh', jnp.einsum('tei,eri->ter', h, down_lora_A), down_lora_B)
        out_sel = jnp.take_along_axis(out, selected[:, :, None], axis=1)
        y = jnp.einsum('tkh,tk->th', out_sel, routing_weights)
        return y.reshape(B, S, H)

    def _L1_attn_ref(hidden_states, w_qkv, k_pos, v_pos, k_cw1, k_cb1, k_cw2, k_cb2, v_cw1, v_cb1, v_cw2, v_cb2, mem_ck, mem_cv, w_gate, b_gate, w_out):
        import jax, jax.numpy as jnp
        import numpy as np
        B, S, DIM = (1, 256, 256)
        HEADS, KV_HEADS = (32, 8)
        DH = DIM // HEADS
        G = HEADS // KV_HEADS
        CBLK = 16
        SBLK = 16
        NSEL = 8
        WIN = 64
        SCALE = DH ** (-0.5)
        NEG = -1e+30
        CDIM = CBLK * DH

        def _rope(x, pos):
            d = x.shape[-1]
            inv = 1.0 / 10000.0 ** (jnp.arange(0, d, 2, dtype=jnp.float32) / d)
            ang = pos[:, None] * inv[None, :]
            cos, sin = (jnp.cos(ang), jnp.sin(ang))
            x1, x2 = (x[..., 0::2], x[..., 1::2])
            return jnp.stack([x1 * cos - x2 * sin, x1 * sin + x2 * cos], axis=-1).reshape(x.shape)

        def _forward(x, w_qkv, k_pos, v_pos, k_cw1, k_cb1, k_cw2, k_cb2, v_cw1, v_cb1, v_cw2, v_cb2, mem_ck, mem_cv, w_gate, b_gate, w_out):
            b, n, _ = x.shape
            di, dkv = (HEADS * DH, KV_HEADS * DH)
            qkv = x @ w_qkv
            q = qkv[..., :di].reshape(b, n, KV_HEADS, G, DH).transpose(0, 2, 3, 1, 4)
            k = qkv[..., di:di + dkv].reshape(b, n, KV_HEADS, DH).transpose(0, 2, 1, 3)
            v = qkv[..., di + dkv:].reshape(b, n, KV_HEADS, DH).transpose(0, 2, 1, 3)
            nc = n // CBLK
            kb = k[:, :, :nc * CBLK].reshape(b, KV_HEADS, nc, CBLK, DH) + k_pos[None, :, None]
            vb = v[:, :, :nc * CBLK].reshape(b, KV_HEADS, nc, CBLK, DH) + v_pos[None, :, None]
            ck = jax.nn.relu(kb.reshape(b, KV_HEADS, nc, CDIM) @ k_cw1 + k_cb1) @ k_cw2 + k_cb2
            cv = jax.nn.relu(vb.reshape(b, KV_HEADS, nc, CDIM) @ v_cw1 + v_cb1) @ v_cw2 + v_cb2
            ck = jnp.concatenate([jnp.broadcast_to(mem_ck[None], (b, KV_HEADS, 1, DH)), ck], axis=2)
            cv = jnp.concatenate([jnp.broadcast_to(mem_cv[None], (b, KV_HEADS, 1, DH)), cv], axis=2)
            csim = jnp.einsum('bhgnd,bhjd->bhgnj', q, ck) * SCALE
            ck_last = jnp.concatenate([jnp.array([-1]), (jnp.arange(nc) + 1) * CBLK - 1])
            cmask = ck_last[None, :] < jnp.arange(n)[:, None]
            csim = jnp.where(cmask, csim, NEG)
            c_out = jnp.einsum('bhgnj,bhjd->bhgnd', jax.nn.softmax(csim, -1), cv)
            imp = csim[..., 1:].mean(axis=2)
            imp = jnp.concatenate([jnp.full(imp.shape[:-1] + (1,), -1000.0, imp.dtype), imp], axis=-1)
            imp = jax.nn.softmax(imp, -1)[..., 1:]
            sel_vals, sel_idx = jax.lax.top_k(imp, NSEL)
            fine_gate_mask = sel_vals > 1e-10
            pos = jnp.arange(n, dtype=jnp.float32)
            rq, rk = (_rope(q, pos), _rope(k, pos))
            nf = n // SBLK
            own = jnp.broadcast_to((jnp.arange(n) // SBLK)[None, None, :, None], (b, KV_HEADS, n, 1))
            idx = jnp.concatenate([sel_idx, own], axis=-1)
            kblocks = rk.reshape(b, KV_HEADS, nf, SBLK, DH)
            vblocks = v.reshape(b, KV_HEADS, nf, SBLK, DH)
            bi = jnp.arange(b)[:, None, None, None]
            hi = jnp.arange(KV_HEADS)[None, :, None, None]
            fk = kblocks[bi, hi, idx].reshape(b, KV_HEADS, n, (NSEL + 1) * SBLK, DH)
            fv = vblocks[bi, hi, idx].reshape(b, KV_HEADS, n, (NSEL + 1) * SBLK, DH)
            sel_m = jnp.repeat(fine_gate_mask[..., None], SBLK, -1).reshape(b, KV_HEADS, n, NSEL * SBLK)
            diag_m = (jnp.arange(n) % SBLK)[:, None] >= jnp.arange(SBLK)[None, :]
            fmask = jnp.concatenate([sel_m, jnp.broadcast_to(diag_m[None, None], (b, KV_HEADS, n, SBLK))], axis=-1)
            fsim = jnp.einsum('bhgnd,bhnjd->bhgnj', rq, fk) * SCALE
            fsim = jnp.where(fmask[:, :, None], fsim, NEG)
            f_out = jnp.einsum('bhgnj,bhnjd->bhgnd', jax.nn.softmax(fsim, -1), fv)
            nwin = n // WIN
            qw = rq.reshape(b, KV_HEADS, G, nwin, WIN, DH)
            kw = rk.reshape(b, KV_HEADS, nwin, WIN, DH)
            vw = v.reshape(b, KV_HEADS, nwin, WIN, DH)
            kcat = jnp.concatenate([jnp.concatenate([jnp.zeros_like(kw[:, :, :1]), kw[:, :, :-1]], 2), kw], 3)
            vcat = jnp.concatenate([jnp.concatenate([jnp.zeros_like(vw[:, :, :1]), vw[:, :, :-1]], 2), vw], 3)
            ssim = jnp.einsum('bhgwid,bhwjd->bhgwij', qw, kcat) * SCALE
            i_, j_ = (jnp.arange(WIN), jnp.arange(2 * WIN))
            delta = i_[:, None] - (j_[None, :] - WIN)
            smask = ((delta >= 0) & (delta <= WIN))[None] & ((jnp.arange(nwin) > 0)[:, None, None] | (j_ >= WIN)[None, None, :])
            ssim = jnp.where(smask[None, None, None], ssim, NEG)
            s_out = jnp.einsum('bhgwij,bhwjd->bhgwid', jax.nn.softmax(ssim, -1), vcat)
            s_out = s_out.reshape(b, KV_HEADS, G, n, DH)
            gates = jax.nn.sigmoid(x @ w_gate + b_gate).reshape(b, n, KV_HEADS, G, 3).transpose(0, 2, 3, 1, 4)
            out = gates[..., 0:1] * c_out + gates[..., 1:2] * f_out + gates[..., 2:3] * s_out
            out = out.transpose(0, 3, 1, 2, 4).reshape(b, n, HEADS * DH)
            return out @ w_out
        return _forward(hidden_states, w_qkv, k_pos, v_pos, k_cw1, k_cb1, k_cw2, k_cb2, v_cw1, v_cb1, v_cw2, v_cb2, mem_ck, mem_cv, w_gate, b_gate, w_out)

    def _L1_ffn_ref(x, ln1_w, ln2_w, kv_d_w, q_d_w, k_u_w, v_u_w, q_u_w, rope_k_w, rope_q_w, o_w, sh_gate, sh_up, sh_down, r_gate, r_up, r_down, router_w, router_b):
        import jax, jax.numpy as jnp
        import numpy as np
        B, S, H = (4, 128, 256)
        NH = 16
        HD = H // NH
        RD = HD // 2
        LAT = H // 4
        I = 128
        NE = 8
        NSH = 1
        NR = NE - NSH
        TOPK = 2
        EPS = 1e-05
        SCALING = 8.0

        def _w(key, shape, fan_in):
            return jax.random.normal(key, shape, dtype=jnp.float32) / np.sqrt(fan_in)

        def rmsnorm(x, w):
            rms = jax.lax.rsqrt(jnp.mean(x * x, axis=-1, keepdims=True) + EPS)
            return w * rms * x

        def rope_cos_sin(seq_len):
            inv_freq = 1.0 / 10000.0 ** (jnp.arange(0, RD, 2, dtype=jnp.float32) / RD)
            t = jnp.arange(seq_len, dtype=jnp.float32)
            ang = jnp.outer(t, inv_freq)
            emb = jnp.concatenate([ang, ang], axis=-1)
            return (jnp.cos(emb), jnp.sin(emb))

        def apply_rope(x, cos, sin):
            c = cos[None, :, None, :]
            s = sin[None, :, None, :]
            x1, x2 = jnp.split(x, 2, axis=-1)
            rot = jnp.concatenate([-x2, x1], axis=-1)
            return x * c + rot * s

        def expert_ffn(x, wg, wu, wd):
            h = jax.nn.silu(x @ wg) * (x @ wu) / SCALING
            return h @ wd

        def attention(x, kv_d_w, q_d_w, k_u_w, v_u_w, q_u_w, rope_k_w, rope_q_w, o_w):
            b, s, _ = x.shape
            kv_d = x @ kv_d_w
            q_d = x @ q_d_w
            k_p = (kv_d @ k_u_w).reshape(b, s, NH, RD)
            q_p = (q_d @ q_u_w).reshape(b, s, NH, RD)
            v = (kv_d @ v_u_w).reshape(b, s, NH, HD)
            k_r = (x @ rope_k_w).reshape(b, s, NH, RD)
            q_r = (q_d @ rope_q_w).reshape(b, s, NH, RD)
            cos, sin = rope_cos_sin(s)
            k_r = apply_rope(k_r, cos, sin)
            q_r = apply_rope(q_r, cos, sin)
            k = jnp.concatenate([k_p, k_r], axis=-1)
            q = jnp.concatenate([q_p, q_r], axis=-1)
            scale = 1.0 / np.sqrt(HD)
            scores = jnp.einsum('bqhd,bkhd->bhqk', q, k) * scale
            causal = jnp.tril(jnp.ones((s, s), dtype=bool))
            scores = jnp.where(causal[None, None], scores, jnp.finfo(scores.dtype).min)
            probs = jax.nn.softmax(scores, axis=-1)
            out = jnp.einsum('bhqk,bkhd->bqhd', probs, v).reshape(b, s, H)
            return out @ o_w

        def moe(x, sh_gate, sh_up, sh_down, r_gate, r_up, r_down, router_w, router_b):
            shared = expert_ffn(x, sh_gate, sh_up, sh_down)
            logits = x @ router_w + router_b
            probs = jax.nn.sigmoid(logits)
            scores, idx = jax.lax.top_k(probs, TOPK)
            scores = scores / jnp.sum(scores, axis=-1, keepdims=True)
            w = jnp.sum(jax.nn.one_hot(idx, NR, dtype=x.dtype) * scores[..., None], axis=-2)
            combined = jnp.zeros_like(x)
            for e in range(NR):
                combined = combined + w[..., e:e + 1] * expert_ffn(x, r_gate[e], r_up[e], r_down[e])
            return shared + combined
        h = x + attention(rmsnorm(x, ln1_w), kv_d_w, q_d_w, k_u_w, v_u_w, q_u_w, rope_k_w, rope_q_w, o_w)
        out = h + moe(rmsnorm(h, ln2_w), sh_gate, sh_up, sh_down, r_gate, r_up, r_down, router_w, router_b)
        return out
    x = L0_attn_x
    x = _layernorm(x + _L0_attn_ref(x, L0_attn_W_in, L0_attn_W_out, L0_attn_dt_bias, L0_attn_A_log, L0_attn_D_param, L0_attn_B_bias, L0_attn_C_bias, L0_attn_rope_freqs, L0_attn_norm_w), axis=-1)
    x = _layernorm(x + _L0_ffn_ref(x, L0_ffn_gate_weight, L0_ffn_gate_lora_A, L0_ffn_gate_lora_B, L0_ffn_gate_up_proj, L0_ffn_down_proj, L0_ffn_gup_lora_A, L0_ffn_gup_lora_B, L0_ffn_down_lora_A, L0_ffn_down_lora_B), axis=-1)
    x = _layernorm(x + _L1_attn_ref(x, L1_attn_w_qkv, L1_attn_k_pos, L1_attn_v_pos, L1_attn_k_cw1, L1_attn_k_cb1, L1_attn_k_cw2, L1_attn_k_cb2, L1_attn_v_cw1, L1_attn_v_cb1, L1_attn_v_cw2, L1_attn_v_cb2, L1_attn_mem_ck, L1_attn_mem_cv, L1_attn_w_gate, L1_attn_b_gate, L1_attn_w_out), axis=-1)
    x = _layernorm(x + _L1_ffn_ref(x, L1_ffn_ln1_w, L1_ffn_ln2_w, L1_ffn_kv_d_w, L1_ffn_q_d_w, L1_ffn_k_u_w, L1_ffn_v_u_w, L1_ffn_q_u_w, L1_ffn_rope_k_w, L1_ffn_rope_q_w, L1_ffn_o_w, L1_ffn_sh_gate, L1_ffn_sh_up, L1_ffn_sh_down, L1_ffn_r_gate, L1_ffn_r_up, L1_ffn_r_down, L1_ffn_router_w, L1_ffn_router_b), axis=-1)
    return x

_drawn_inputs = setup_inputs


def setup_inputs(seed=0):
    import zlib

    import numpy as np

    out = dict(_drawn_inputs(seed))
    spreads = {'L0_attn_D_param': (1.0, 0.2),
     'L0_attn_norm_w': (1.0, 0.2),
     'L1_attn_k_cb1': (0.0, 0.8),
     'L1_attn_k_cb2': (0.0, 0.8),
     'L1_attn_v_cb1': (0.0, 0.8),
     'L1_attn_v_cb2': (0.0, 0.8),
     'L1_ffn_ln1_w': (1.0, 0.548),
     'L1_ffn_ln2_w': (1.0, 0.6),
     'L1_ffn_router_b': (0.0, 0.8)}
    factors = {'L0_ffn_down_lora_A': 3.853,
     'L0_ffn_down_lora_B': 3.868,
     'L1_attn_w_qkv': 3.925,
     'L1_attn_k_pos': 8.0,
     'L1_attn_v_pos': 8.0,
     'L1_attn_k_cw1': 8.0,
     'L1_attn_k_cw2': 8.0,
     'L1_attn_v_cw1': 8.0,
     'L1_attn_v_cw2': 8.0,
     'L1_attn_mem_ck': 55.633,
     'L1_attn_mem_cv': 27.76,
     'L1_attn_w_gate': 8.0,
     'L1_attn_w_out': 3.816}
    for name, (base, spread) in spreads.items():
        noise = np.random.default_rng([zlib.crc32(name.encode()), seed]).standard_normal(out[name].shape)
        drawn = base * np.exp(spread * noise) if base else spread * noise
        out[name] = jnp.asarray(drawn.astype(out[name].dtype))
    for name, factor in factors.items():
        out[name] = (out[name] * factor).astype(out[name].dtype)
    return out
```

```python
from contextlib import ExitStack, contextmanager

import numpy as np

import concourse.bass as bass
from concourse import mybir

ALU = mybir.AluOpType
ACT = mybir.ActivationFunctionType
AX = mybir.AxisListType.X
F32 = mybir.dt.float32
BF16 = mybir.dt.bfloat16
U32 = mybir.dt.uint32

P = 128
BATCH, T, D = 4, 1024, 256
NT = T // P
KD = D // P
LN_EPS = 1e-5


class Cursor:

    def __init__(self, eng, sem):
        self.eng, self.sem, self.base, self.n = eng, sem, 0, 0

    def next(self, k=1):
        self.n += k
        return self.base + self.n


def stage_semaphores(nc, ctx, tag, names):
    s = {n: nc.alloc_semaphore(tag + n) for n in names}

    def give_back():
        nc.clear_and_free_semaphores(list(s.values()))
        nc.all_engine_barrier()

    ctx.callback(give_back)
    return s


@contextmanager
def loop(eng, count, *cursors):
    outer = [(c.base, c.n) for c, _ in cursors]
    with eng.Fori(0, count) as i:
        for (c, per), (base, n) in zip(cursors, outer):
            c.base, c.n = base + n + i * per, 0
        yield i
        for k, (c, per) in enumerate(cursors):
            assert c.n == per, f"cursor {k} ({c.sem}): {c.n} signals in an iteration, not {per}"
    for (c, per), (base, n) in zip(cursors, outer):
        c.base, c.n = base, n + count * per


def moe_stage(nc, x_in, res_in, x_out, router, gate_up, down, lora=None, rms_w=None, router_b=None):
    E, I, R = 8, 128, 16
    SCALING = 8.0
    NRT = router.shape[1]
    GROUP = 512
    NG = BATCH * T // GROUP
    TPG = GROUP // P
    SIG = router_b is not None
    with ExitStack() as ctx:
        def sb(name, shape, dt=F32):
            return ctx.enter_context(nc.sbuf_tensor(name, shape, dt))

        s = stage_semaphores(nc, ctx, "", ())

        def sem(name):
            s[name] = nc.alloc_semaphore(name)
            return s[name]

        tag = "m1_" if SIG else "m0_"
        xT = sb(tag + "xT", [P, KD, BATCH * T])
        Y = sb(tag + "Y", [P, BATCH * NT, D])
        xin = [sb(tag + f"xin{i}", [P, NT, D]) for i in range(2)]
        ident = sb(tag + "ident", [P, P])
        iota8 = sb(tag + "iota8", [P, E])
        routerT = sb(tag + "routerT", [P, KD, NRT])
        lgT = sb(tag + "lgT", [NRT, T])
        lg = sb(tag + "lg", [P, NT, E])
        top = sb(tag + "top", [P, NT, 8])
        topi = sb(tag + "topi", [P, NT, 8], U32)
        topf = sb(tag + "topf", [P, NT, 2])
        sc = sb(tag + "sc", [P, NT, 4])
        oh = sb(tag + "oh", [P, 2, NT, E])
        Wt = sb(tag + "Wt", [P, BATCH * NT, E])
        wraw = [sb(tag + f"wraw{i}", [P, KD, 2 * I]) for i in range(2)]
        draw = [sb(tag + f"draw{i}", [P, D]) for i in range(2)]
        sg = [sb(tag + f"sg{i}", [P, GROUP]) for i in range(2)]
        hT = [sb(tag + f"hT{i}", [P, GROUP]) for i in range(2)]
        stats = sb(tag + "stats", [P, NT, 6])
        mv = sb(tag + "mv", [P, NT, 2])
        rs = sb(tag + "rs", [P, NT, 1])
        eps = sb(tag + "eps", [P, 1])
        lnw = sb(tag + "lnw", [P, D]) if SIG else None
        sq = sb(tag + "sq", [P, NT, D]) if SIG else None
        rb = sb(tag + "rb", [P, NRT]) if SIG else None
        if lora:
            gA = [sb(tag + f"gA{i}", [R, D]) for i in range(2)]
            gB = [sb(tag + f"gB{i}", [R, 2 * I]) for i in range(2)]
            dA = [sb(tag + f"dA{i}", [R, I]) for i in range(2)]
            dB = [sb(tag + f"dB{i}", [R, D]) for i in range(2)]
            rA = sb(tag + "rA", [R, D])
            rBT = sb(tag + "rBT", [R, NRT])
        ps = [ctx.enter_context(nc.psum_tensor(tag + f"ps{i}", [P, 512], F32)) for i in range(8)]

        s_apart = sem(tag + "apart")
        s_const = sem(tag + "const_ready")
        s_cdma = sem(tag + "const_loaded")
        s_router = sem(tag + "router_folded")
        s_rfold = sem(tag + "router_fold_product")
        s_xin = [sem(tag + f"x_loaded{i}") for i in range(2)]
        s_xfree = sem(tag + "x_buffer_free")
        s_norm = sem(tag + "x_normed")
        s_tr = sem(tag + "x_transposed")
        s_trc = sem(tag + "xT_copied")
        s_lgT = sem(tag + "logitsT_ready")
        s_lgTc = sem(tag + "logitsT_copied")
        s_lg = sem(tag + "logits_ready")
        s_lgfree = sem(tag + "logits_bank_free")
        s_exp = sem(tag + "route_exp_ready")
        s_dif = sem(tag + "route_arg_ready")
        s_w = [sem(tag + f"weights_loaded{i}") for i in range(2)]
        s_wfree = sem(tag + "weights_buffer_free")
        s_fold = sem(tag + "fold_product")
        s_folded = sem(tag + "weights_folded")
        s_up = sem(tag + "gate_up_ready")
        s_silu = sem(tag + "silu_ready")
        s_h = sem(tag + "h_ready")
        s_down = sem(tag + "down_ready")
        s_acc = sem(tag + "accumulated")
        s_nvar = sem(tag + "norm_square_sum_ready")
        s_nstd = sem(tag + "norm_root_ready")
        s_var = sem(tag + "variance_ready")
        s_std = sem(tag + "std_ready")
        s_res = sem(tag + "result_ready")
        s_store = [sem(tag + f"result_stored{i}") for i in range(2)]
        s_dve = sem(tag + "dve_own")
        s_act = sem(tag + "act_own")
        s_pool = sem(tag + "pool_own")
        x_v = x_in.rearrange("(b c p) d -> b p c d", p=P, c=NT)
        r_v = res_in.rearrange("(b c p) d -> b p c d", p=P, c=NT)
        o_v = x_out.rearrange("(b c p) d -> b p c d", p=P, c=NT)
        n_const = 3 + (2 if SIG else 0) + (2 if lora else 0)
        n_w = 2 + (4 if lora else 0)
        with nc.Block() as block:

            @block.gpsimd
            def _(pool):
                own = Cursor(pool, s_pool)
                pool.memset(ident[:, :], 0.0).then_inc(s_pool, 1)
                pool.wait_ge(s_pool, own.next())
                pool.affine_select(out=ident[:, :], in_=ident[:, :], compare_op=ALU.not_equal,
                                   fill=1.0, base=0, pattern=[[-1, P]], channel_multiplier=1).then_inc(s_pool, 1)
                pool.wait_ge(s_pool, own.next())
                pool.iota(iota8[:, :], pattern=[[1, E]], base=0, channel_multiplier=0,
                          allow_small_or_imprecise_dtypes=True).then_inc(s_pool, 1)
                pool.wait_ge(s_pool, own.next())
                pool.memset(eps[:, :], LN_EPS).then_inc(s_pool, 1)
                pool.wait_ge(s_pool, own.next())
                pool.memset(lg[:, :, :], -3e38).then_inc(s_const, 1)

            @block.sync
            def _(sp):
                sp.dma_start(routerT[:, :, :], router.rearrange("(k p) e -> p k e", p=P)).then_inc(s_cdma, 16)
                if SIG:
                    sp.dma_start(lnw[:, :], rms_w.partition_broadcast(P)).then_inc(s_cdma, 16)
                    sp.dma_start(rb[:, :], router_b.partition_broadcast(P)).then_inc(s_cdma, 16)
                if lora:
                    sp.dma_start(rA[:, :], lora["rA"]).then_inc(s_cdma, 16)
                    sp.dma_start(rBT[:, :], lora["rBT"]).then_inc(s_cdma, 16)
                free, wfree, res = Cursor(sp, s_xfree), Cursor(sp, s_wfree), Cursor(sp, s_res)
                with loop(sp, BATCH // 2, (free, 2)) as b2:
                    for par in range(2):
                        sp.wait_ge(s_xfree, free.next())
                        sp.dma_start(xin[par][:, :, :], x_v[b2 * 2 + par]).then_inc(s_xin[par], 16)
                with loop(sp, E // 2, (wfree, 2)) as e2:
                    for par in range(2):
                        sp.wait_ge(s_wfree, wfree.next())
                        e = e2 * 2 + par
                        sp.dma_start(wraw[par][:, :, :], gate_up[e]).then_inc(s_w[par], 16)
                        sp.dma_start(draw[par][:, :], down[e]).then_inc(s_w[par], 16)
                        if lora:
                            sp.dma_start(gA[par][:, :], lora["gA"][e]).then_inc(s_w[par], 16)
                            sp.dma_start(gB[par][:, :], lora["gB"][e]).then_inc(s_w[par], 16)
                            sp.dma_start(dA[par][:, :], lora["dA"][e]).then_inc(s_w[par], 16)
                            sp.dma_start(dB[par][:, :], lora["dB"][e]).then_inc(s_w[par], 16)
                stored = [Cursor(sp, x) for x in s_store]
                with loop(sp, BATCH // 2, (free, 2), (res, 2), (stored[0], 16), (stored[1], 16)) as b2:
                    for par in range(2):
                        sp.wait_ge(s_xfree, free.next())
                        sp.dma_start(xin[par][:, :, :], r_v[b2 * 2 + par]).then_inc(s_xin[par], 16)
                    for par in range(2):
                        sp.wait_ge(s_res, res.next())
                        sp.dma_start(o_v[b2 * 2 + par], xin[par][:, :, :]).then_inc(s_store[par], 16)
                        sp.wait_ge(s_store[par], stored[par].next(16))
                        sp.sem_inc(s_xfree, 1)

            def banks(j):
                return ps[j % 4]

            @block.tensor
            def _(pe):
                xl, nrm, trc = [Cursor(pe, x) for x in s_xin], Cursor(pe, s_norm), Cursor(pe, s_trc)
                lgTc, lgfree = Cursor(pe, s_lgTc), Cursor(pe, s_lgfree)
                pe.wait_ge(s_const, 1)
                pe.wait_ge(s_cdma, 16 * (n_const - 2))
                if lora:
                    for k in range(KD):
                        mm = pe.matmul(ps[7][:, k * NRT:(k + 1) * NRT], rA[:, k * P:(k + 1) * P], rBT[:, :],
                                       start=True, stop=True)
                    mm.then_inc(s_rfold, 1)
                pe.wait_ge(s_router, 1)
                with loop(pe, BATCH // 2, (xl[0], 0 if SIG else 16), (xl[1], 0 if SIG else 16),
                          (nrm, 2 if SIG else 0), (trc, 8), (lgTc, 4), (lgfree, 2)) as b2:
                    for par in range(2):
                        if SIG:
                            pe.wait_ge(s_norm, nrm.next())
                        else:
                            pe.wait_ge(s_xin[par], xl[par].next(16))
                        for j in range(4):
                            k, h = j // 2, j % 2
                            pe.wait_ge(s_trc, trc.next())
                            for c in range(4):
                                mm = pe.transpose(banks(j)[:, c * P:(c + 1) * P],
                                                  xin[par][:, h * 4 + c, k * P:(k + 1) * P], ident[:, :])
                            mm.then_inc(s_tr, 1)
                        pe.wait_ge(s_trc, (b2 * 2 + par + 1) * 4 + 4)
                        for h in range(2):
                            pe.wait_ge(s_lgTc, lgTc.next())
                            for k in range(KD):
                                mm = pe.matmul(ps[4 + h][0:NRT, :], routerT[:, k, :],
                                               xT[:, k, bass.ds((b2 * 2 + par) * T + h * 512, 512)],
                                               start=(k == 0), stop=(k == KD - 1))
                            mm.then_inc(s_lgT, 1)
                        pe.wait_ge(s_lgTc, (b2 * 2 + par + 1) * 2 + 2)
                        pe.wait_ge(s_lgfree, lgfree.next())
                        pe.sem_inc(s_apart, 1)
                        for c in range(NT):
                            mm = pe.transpose(ps[6][:, c * NRT:(c + 1) * NRT], lgT[:, c * P:(c + 1) * P],
                                              ident[0:NRT, 0:NRT])
                        mm.then_inc(s_lg, 1)
                pe.wait_ge(s_lgfree, lgfree.next())
                pe.sem_inc(s_apart, 1)
                wl = [Cursor(pe, x) for x in s_w]
                folded, hrd, acc = (Cursor(pe, x) for x in (s_folded, s_h, s_acc))
                with loop(pe, E // 2, (wl[0], 16 * n_w), (wl[1], 16 * n_w), (folded, 2), (hrd, 2 * NG),
                          (acc, 4 * NG)) as e2:
                    for par in range(2):
                        pe.wait_ge(s_w[par], wl[par].next(16 * n_w))
                        if lora:
                            for k in range(KD):
                                pe.matmul(ps[6][:, k * 2 * I:(k + 1) * 2 * I], gA[par][:, k * P:(k + 1) * P],
                                          gB[par][:, :], start=True, stop=True)
                            pe.matmul(ps[7][:, 0:D], dA[par][:, :], dB[par][:, :],
                                      start=True, stop=True).then_inc(s_fold, 1)
                            pe.wait_ge(s_folded, folded.next())
                            pe.sem_inc(s_apart, 1)
                        else:
                            folded.n += 1
                            pe.sem_inc(s_apart, 1)
                        with loop(pe, NG // 2, (hrd, 2), (acc, 4)) as g2:
                            for q in range(2):
                                for half in range(2):
                                    for k in range(KD):
                                        mm = pe.matmul(ps[2 * q + half][:, :],
                                                       wraw[par][:, k, half * I:(half + 1) * I],
                                                       xT[:, k, bass.ds((g2 * 2 + q) * GROUP, GROUP)],
                                                       start=(k == 0), stop=(k == KD - 1))
                                mm.then_inc(s_up, 1)
                            for q in range(2):
                                pe.wait_ge(s_h, hrd.next())
                                for d in range(2):
                                    pe.wait_ge(s_acc, acc.next())
                                    for c in range(2):
                                        mm = pe.matmul(ps[4 + d][:, c * D:(c + 1) * D],
                                                       hT[q][:, (2 * d + c) * P:(2 * d + c + 1) * P],
                                                       draw[par][:, :], start=True, stop=True)
                                    mm.then_inc(s_down, 1)

            @block.scalar
            def _(act):
                tr, lgTr, dif = Cursor(act, s_tr), Cursor(act, s_lgT), Cursor(act, s_dif)
                nvar = Cursor(act, s_nvar)
                act.wait_ge(s_const, 1)
                with loop(act, BATCH // 2, (tr, 8), (lgTr, 4), (dif, 2), (nvar, 2 if SIG else 0)) as b2:
                    for par in range(2):
                        if SIG:
                            act.wait_ge(s_nvar, nvar.next())
                            act.activation(rs[:, :, :], mv[:, :, 0:1], ACT.Sqrt, bias=eps[:, 0:1],
                                           scale=1.0 / D).then_inc(s_nstd, 1)
                        for j in range(4):
                            k, h = j // 2, j % 2
                            act.wait_ge(s_tr, tr.next())
                            act.copy(xT[:, k, bass.ds((b2 * 2 + par) * T + h * 512, 512)],
                                     banks(j)[:, :]).then_inc(s_trc, 1)
                        for h in range(2):
                            act.wait_ge(s_lgT, lgTr.next())
                            act.copy(lgT[:, h * 512:(h + 1) * 512], ps[4 + h][0:NRT, :]).then_inc(s_lgTc, 1)
                        act.wait_ge(s_dif, dif.next())
                        if SIG:
                            act.activation(sc[:, :, 1:3], top[:, :, 0:2], ACT.Sigmoid).then_inc(s_exp, 1)
                        else:
                            act.activation(sc[:, :, 1:2], sc[:, :, 0:1], ACT.Exp).then_inc(s_exp, 1)
                up, hrd = Cursor(act, s_up), Cursor(act, s_h)
                with loop(act, E * NG // 2, (up, 2), (hrd, 2)) as n2:
                    for q in range(2):
                        act.wait_ge(s_up, up.next())
                        act.activation(sg[q][:, :], ps[2 * q][:, :], ACT.Silu).then_inc(s_silu, 1)
                        hrd.n += 1
                var = Cursor(act, s_var)
                with loop(act, BATCH, (var, 1)) as b:
                    act.wait_ge(s_var, var.next())
                    act.activation(rs[:, :, :], mv[:, :, 1:2], ACT.Sqrt, bias=eps[:, 0:1]).then_inc(s_std, 1)

            @block.vector
            def _(dve):
                own = Cursor(dve, s_dve)
                dve.wait_ge(s_const, 1)
                if lora:
                    dve.wait_ge(s_rfold, 1)
                    dve.wait_ge(s_cdma, 16 * (n_const - 2))
                    dve.scalar_tensor_tensor(
                        out=routerT[:, :, :], in0=ps[7][:, 0:KD * NRT].rearrange("p (k e) -> p k e", k=KD),
                        scalar=2.0, in1=routerT[:, :, :], op0=ALU.mult, op1=ALU.add).then_inc(s_dve, 1)
                    dve.wait_ge(s_dve, own.next())
                    dve.sem_inc(s_router, 1)
                else:
                    dve.wait_ge(s_cdma, 16 * (n_const - 2))
                    dve.sem_inc(s_router, 1)
                dve.sem_inc(s_xfree, 2)
                dve.sem_inc(s_wfree, 2)
                dve.sem_inc(s_trc, 4)
                dve.sem_inc(s_lgTc, 2)
                dve.sem_inc(s_acc, 2)
                dve.sem_inc(s_lgfree, 1)
                nstd = Cursor(dve, s_nstd)
                xl = [Cursor(dve, x) for x in s_xin]
                lgr, ex = Cursor(dve, s_lg), Cursor(dve, s_exp)
                with loop(dve, BATCH // 2, (xl[0], 16), (xl[1], 16), (lgr, 2), (ex, 2), (own, 2 * (16 if SIG else 13)),
                          (nstd, 2 if SIG else 0)) as b2:
                    for par in range(2):
                        dve.wait_ge(s_xin[par], xl[par].next(16))
                        if SIG:
                            X = xin[par]
                            dve.tensor_tensor(sq[:, :, :], X[:, :, :], X[:, :, :], ALU.mult).then_inc(s_dve, 1)
                            dve.wait_ge(s_dve, own.next())
                            dve.tensor_reduce(mv[:, :, 0:1], sq[:, :, :], AX, ALU.add).then_inc(s_nvar, 1)
                            dve.wait_ge(s_nstd, nstd.next())
                            dve.reciprocal(rs[:, :, :], rs[:, :, :]).then_inc(s_dve, 1)
                            dve.wait_ge(s_dve, own.next())
                            dve.tensor_tensor(X[:, :, :], X[:, :, :],
                                              rs[:, :, :].broadcast_to([P, NT, D]), ALU.mult).then_inc(s_dve, 1)
                            dve.wait_ge(s_dve, own.next())
                            dve.tensor_tensor(X[:, :, :], X[:, :, :], lnw[:, :].rearrange(
                                  "p (o d) -> p o d", o=1).broadcast_to([P, NT, D]), ALU.mult).then_inc(s_dve, 1)
                            dve.wait_ge(s_dve, own.next())
                            dve.sem_inc(s_norm, 1)
                        dve.wait_ge(s_lg, lgr.next())
                        lgp = ps[6][:, 0:NT * NRT].rearrange("p (c e) -> p c e", e=NRT)
                        dve.sem_inc(s_xfree, 1)
                        if SIG:
                            dve.tensor_tensor(lg[:, :, 0:NRT], lgp,
                                              rb[:, :].rearrange("p (o e) -> p o e", o=1).broadcast_to([P, NT, NRT]), ALU.add)\
                               .then_inc(s_dve, 1)
                            dve.wait_ge(s_dve, own.next())
                            dve.sem_inc(s_apart, 1)
                        else:
                            dve.tensor_copy(lg[:, :, 0:NRT], lgp).then_inc(s_dve, 1)
                            dve.wait_ge(s_dve, own.next())
                            dve.sem_inc(s_apart, 1)
                        dve.sem_inc(s_lgfree, 1)
                        for c in range(NT):
                            ins = dve.max(top[:, c, :], lg[:, c, :])
                        ins.then_inc(s_dve, 1)
                        dve.wait_ge(s_dve, own.next())
                        dve.sem_inc(s_apart, 1)
                        for c in range(NT):
                            ins = dve.max_index(topi[:, c, :], top[:, c, :], lg[:, c, :])
                        ins.then_inc(s_dve, 1)
                        dve.wait_ge(s_dve, own.next())
                        if SIG:
                            dve.sem_inc(s_dif, 1)
                        else:
                            dve.tensor_sub(sc[:, :, 0:1], top[:, :, 1:2], top[:, :, 0:1]).then_inc(s_dif, 1)
                        dve.tensor_copy(topf[:, :, :], topi[:, :, 0:2]).then_inc(s_dve, 1)
                        dve.wait_ge(s_dve, own.next())
                        dve.wait_ge(s_exp, ex.next())
                        if SIG:
                            dve.tensor_add(sc[:, :, 0:1], sc[:, :, 1:2], sc[:, :, 2:3]).then_inc(s_dve, 1)
                            dve.wait_ge(s_dve, own.next())
                        else:
                            dve.tensor_scalar_add(sc[:, :, 0:1], sc[:, :, 1:2], 1.0).then_inc(s_dve, 1)
                            dve.wait_ge(s_dve, own.next())
                            dve.memset(sc[:, :, 2:3], 1.0).then_inc(s_dve, 1)
                            dve.wait_ge(s_dve, own.next())
                        dve.reciprocal(sc[:, :, 3:4], sc[:, :, 0:1]).then_inc(s_dve, 1)
                        dve.wait_ge(s_dve, own.next())
                        first, second = (1, 2) if SIG else (2, 1)
                        for r, col in enumerate((first, second)):
                            dve.tensor_tensor(
                                oh[:, r, :, :], iota8[:, :].rearrange("p (o e) -> p o e", o=1).broadcast_to([P, NT, E]),
                                topf[:, :, r:r + 1].broadcast_to([P, NT, E]), ALU.is_equal).then_inc(s_dve, 1)
                            dve.wait_ge(s_dve, own.next())
                            dve.tensor_tensor(oh[:, r, :, :], oh[:, r, :, :],
                                              sc[:, :, col:col + 1].broadcast_to([P, NT, E]), ALU.mult)\
                               .then_inc(s_dve, 1)
                            dve.wait_ge(s_dve, own.next())
                        dve.tensor_add(oh[:, 0, :, :], oh[:, 0, :, :], oh[:, 1, :, :]).then_inc(s_dve, 1)
                        dve.wait_ge(s_dve, own.next())
                        dve.tensor_tensor(Wt[:, bass.ds((b2 * 2 + par) * NT, NT), :], oh[:, 0, :, :],
                                          sc[:, :, 3:4].broadcast_to([P, NT, E]), ALU.mult).then_inc(s_dve, 1)
                        dve.wait_ge(s_dve, own.next())
                if SIG:
                    dve.memset(Wt[:, :, E - 1:], 1.0).then_inc(s_dve, 1)
                    dve.wait_ge(s_dve, own.next())
                    dve.tensor_scalar(Wt[:, :, :], Wt[:, :, :], 1.0 / SCALING, None, ALU.mult).then_inc(s_dve, 1)
                    dve.wait_ge(s_dve, own.next())
                dve.memset(Y[:, :, :], 0.0).then_inc(s_dve, 1)
                dve.wait_ge(s_dve, own.next())
                wl = [Cursor(dve, x) for x in s_w]
                fold, silu, down = (Cursor(dve, x) for x in (s_fold, s_silu, s_down))
                with loop(dve, E // 2, (wl[0], 16 * n_w), (wl[1], 16 * n_w), (fold, 2), (silu, 2 * NG),
                          (down, 4 * NG)) as e2:
                    for par in range(2):
                        dve.wait_ge(s_w[par], wl[par].next(16 * n_w))
                        fold.n += 1
                        if lora:
                            dve.wait_ge(s_fold, e2 * 2 + par + 1)
                            dve.scalar_tensor_tensor(
                                out=wraw[par][:, :, :], in0=ps[6][:, :].rearrange("p (k e) -> p k e", k=KD),
                                scalar=2.0, in1=wraw[par][:, :, :], op0=ALU.mult, op1=ALU.add)
                            dve.scalar_tensor_tensor(
                                out=draw[par][:, :], in0=ps[7][:, 0:D],
                                scalar=2.0, in1=draw[par][:, :], op0=ALU.mult, op1=ALU.add).then_inc(s_folded, 1)
                        else:
                            dve.sem_inc(s_apart, 1)
                        with loop(dve, NG // 2, (silu, 2), (down, 4)) as g2:
                            for q in range(2):
                                dve.wait_ge(s_silu, silu.next())
                                dve.tensor_tensor(hT[q][:, :], sg[q][:, :], ps[2 * q + 1][:, :],
                                                  ALU.mult).then_inc(s_h, 1)
                            for q in range(2):
                                for d in range(2):
                                    dve.wait_ge(s_down, down.next())
                                    for c in range(2):
                                        t = (g2 * 2 + q) * TPG + 2 * d + c
                                        yt = Y[:, bass.ds(t, 1), :]
                                        ins = dve.scalar_tensor_tensor(
                                            out=yt, in0=ps[4 + d][:, c * D:(c + 1) * D].rearrange("p (o d) -> p o d", o=1),
                                            scalar=Wt[:, bass.ds(t, 1), bass.ds(e2 * 2 + par, 1)],
                                            in1=yt, op0=ALU.mult, op1=ALU.add)
                                    ins.then_inc(s_acc, 1)
                        dve.sem_inc(s_wfree, 1)
                std = Cursor(dve, s_std)
                with loop(dve, BATCH // 2, (xl[0], 16), (xl[1], 16), (std, 2), (own, 2 * 4)) as b2:
                    for par in range(2):
                        dve.wait_ge(s_xin[par], xl[par].next(16))
                        X = xin[par]
                        dve.tensor_tensor(X[:, :, :], X[:, :, :],
                                          Y[:, bass.ds((b2 * 2 + par) * NT, NT), :], ALU.add).then_inc(s_dve, 1)
                        dve.wait_ge(s_dve, own.next())
                        for c in range(NT):
                            ins = dve.bn_stats(stats[:, c, :], X[:, c, :])
                        ins.then_inc(s_dve, 1)
                        dve.wait_ge(s_dve, own.next())
                        dve.sem_inc(s_apart, 1)
                        for c in range(NT):
                            ins = dve.bn_aggr(mv[:, c, :], stats[:, c, :])
                        ins.then_inc(s_var, 1)
                        dve.wait_ge(s_std, std.next())
                        dve.reciprocal(rs[:, :, :], rs[:, :, :]).then_inc(s_dve, 1)
                        dve.wait_ge(s_dve, own.next())
                        dve.tensor_tensor(X[:, :, :], X[:, :, :],
                                          mv[:, :, 0:1].broadcast_to([P, NT, D]), ALU.subtract).then_inc(s_dve, 1)
                        dve.wait_ge(s_dve, own.next())
                        dve.tensor_tensor(X[:, :, :], X[:, :, :],
                                          rs[:, :, :].broadcast_to([P, NT, D]), ALU.mult).then_inc(s_res, 1)



NEG = -1e30
FAR = -1e15


def causal_scores():
    return [(i, 4 * part, min(i + 1 - 4 * part, 4), part) for i in range(NT) for part in range(i // 4 + 1)]


def causal_probs():
    return [(j, max(j, 4 * h), 4 * h + 4 - max(j, 4 * h)) for j in range(NT) for h in range(j // 4, 2)]


def causal_block(j, i):
    return sum(NT - a for a in range(j)) + i - j


class Attention:

    def __init__(self, nc, ctx, tag, rows, qk_rows, dv, window, masks):
        def sb(name, shape, dt=F32):
            return ctx.enter_context(nc.sbuf_tensor(tag + name, shape, dt))

        self.R, self.RW, self.DV, self.window = rows, qk_rows, dv, window
        self.qst = [sb(f"qst{i}", [P, NT, P], BF16) for i in range(2)]
        self.kst = [sb(f"kst{i}", [P, NT, P], BF16) for i in range(2)]
        self.QT = [sb(f"QT{i}", [P, T], BF16) for i in range(2)]
        self.KT = [sb(f"KT{i}", [P, T], BF16) for i in range(2)]
        self.V = sb("V", [P, NT, masks["heads"], dv + 1])
        self.PT = sb("PT", [P, 36, P])
        self.nb = 2 if window else 1
        self.mp = sb("mp", [P, 2, self.nb, NT])
        self.nm = sb("nm", [P, self.nb, NT])
        self.rem = sb("rem", [P, self.nb, NT])
        self.mb = sb("mb", [P, 2, self.nb, NT], BF16)
        self.MR = 2 * self.nb * NT
        self.Mt = [sb(f"Mt{i}", [self.MR, NT, P], BF16) for i in range(self.nb)]
        self.Vst = [sb(f"Vst{i}", [P, NT, dv + 1]) for i in range(2)]
        self.OR = (self.nb - 1) * 64 + 32 + dv + 1
        self.Orows = sb("Orows", [self.OR, 512])
        self.rden = sb("rden", [P, self.nb, NT, 1])
        if window:
            self.PW = sb("PW", [P, NT, 2, P])
        self.ident = masks["ident"]
        self.identf = masks["identf"]
        self.ones = masks["ones"]
        self.rowmask = masks["rowmask"]
        self.mask = masks["mask"]
        self.ps = masks["ps"]
        names = ("staged Q_turned K_turned Q_copied K_copied max_split maxT_ready Mt_ready S_ready S_taken ST_ready "
                 "P_ready PV_ready PV_copied out_turned PV_taken own_dve own_act own_pool apart").split()
        self.s = stage_semaphores(nc, ctx, tag, names)


    def pe_cursors(self, pe):
        self.pe = pe
        self.pc = {n: Cursor(pe, self.s[n]) for n in
                   ("staged", "Q_copied", "K_copied", "max_split", "Mt_ready", "S_taken", "P_ready", "PV_taken", "PV_copied")}

    def pe_turn(self, q):
        pe = self.pe
        self.pe.wait_ge(self.s["staged"], self.pc["staged"].next())
        self.pe.sem_inc(self.s["apart"], 1)
        for n, (st, side) in enumerate(((self.qst, "Q"), (self.kst, "K"))):
            pe.wait_ge(self.s[side + "_copied"], self.pc[side + "_copied"].next())
            out = self.ps[n].bitcast_bf16
            for c in range(NT):
                mm = pe.transpose(out[0:self.R, c * P:(c + 1) * P], st[q][:, c, 0:self.R], self.ident[:, :])
            mm.then_inc(self.s[side + "_turned"], 1)

    def pe_maxT(self):
        self.pe.wait_ge(self.s["max_split"], self.pc["max_split"].next())
        self.pe.sem_inc(self.s["apart"], 1)
        self.pe.transpose(self.ps[2].bitcast_bf16[0:self.MR, 0:P],
                          self.mb[:, :, :, :].rearrange("p a b c -> p (a b c)"),
                          self.ident[:, :]).then_inc(self.s["maxT_ready"], 1)

    def pe_score_pieces(self):
        return len(causal_scores()) + (NT // 2 if self.window else 0)

    def pe_scores_piece(self, q, n):
        pe, QT, KT, mask, ident = self.pe, self.QT[q], self.KT[q], self.mask, self.ident
        bank = self.ps[3 + n % 2].f32
        pe.wait_ge(self.s["S_taken"], self.pc["S_taken"].next())
        causal = causal_scores()
        if n < len(causal):
            i, k0, kn, part = causal[n]
            diag = k0 + kn - 1 == i
            mm = pe.matmul(bank[:, 0:kn * P], QT[0:self.R, i * P:(i + 1) * P], KT[0:self.R, k0 * P:(k0 + kn) * P],
                           start=True, stop=not diag)
            if diag:
                mm = pe.matmul(bank[:, (kn - 1) * P:kn * P], ident[:, :], mask[:, 0, :], start=False, stop=True)
        else:
            for a in range(2):
                i = 2 * (n - len(causal)) + a
                queries = QT[0:self.RW, i * P:(i + 1) * P]
                if i == 0:
                    for e in range(2):
                        out = bank[:, e * P:(e + 1) * P]
                        pe.matmul(out, queries, KT[0:self.RW, 0:P], start=True, stop=False)
                        mm = pe.matmul(out, ident[:, :], mask[:, 6 - e, :], start=False, stop=True)
                else:
                    out = bank[:, 2 * a * P:2 * (a + 1) * P]
                    pe.matmul(out, queries, KT[0:self.RW, (i - 1) * P:(i + 1) * P], start=True, stop=False)
                    mm = pe.matmul(out, ident[:, :], mask[:, 4:6, :], start=False, stop=True)
        mm.then_inc(self.s["S_ready"], 1)

    def pe_scores(self, q, copied):
        self.pe.wait_ge(self.s["Q_copied"], copied)
        self.pe.wait_ge(self.s["K_copied"], copied)
        for n in range(self.pe_score_pieces()):
            self.pe_scores_piece(q, n)

    def pe_probs_piece(self, q, n):
        pe, QT, KT, mask, ident = self.pe, self.QT[q], self.KT[q], self.mask, self.ident
        bank = self.ps[5 + n % 2].f32
        pe.wait_ge(self.s["P_ready"], self.pc["P_ready"].next())
        causal = causal_probs()
        if n < len(causal):
            j, t0, tn = causal[n]
            out = bank[:, 0:tn * P]
            pe.matmul(out, KT[0:self.R, j * P:(j + 1) * P], QT[0:self.R, t0 * P:(t0 + tn) * P],
                      start=True, stop=False)
            mm = pe.matmul(out, self.ones[:, :], self.Mt[0][:, t0:t0 + tn, :], start=False, stop=t0 != j)
            if t0 == j:
                mm = pe.matmul(bank[:, 0:P], ident[:, :], mask[:, 1, :], start=False, stop=True)
        else:
            for a in range(2):
                j = 2 * (n - len(causal)) + a
                w = min(NT - j, 2)
                out = bank[:, 2 * a * P:(2 * a + w) * P]
                pe.matmul(out, KT[0:self.RW, j * P:(j + 1) * P], QT[0:self.RW, j * P:(j + w) * P],
                          start=True, stop=False)
                pe.matmul(out, self.ones[:, :], self.Mt[1][:, j:j + w, :], start=False, stop=False)
                mm = pe.matmul(out, ident[:, :], mask[:, 2:2 + w, :], start=False, stop=True)
        mm.then_inc(self.s["ST_ready"], 1)

    def pe_values_piece(self, q, n):
        pe, W = self.pe, self.DV + 1
        causal = causal_probs()
        bank = self.ps[7].f32
        if n < len(causal):
            j, t0, tn = causal[n]
            h, c = t0 // 4, t0 % 4
            o = causal_block(j, t0)
            mm = pe.matmul(bank[32 * h:32 * h + W, c * P:(c + tn) * P], self.Vst[q][:, j, :], self.PT[:, o:o + tn, :],
                           start=j == 0, stop=j == 4 * h + 3)
        else:
            for j in (2 * (n - len(causal)), 2 * (n - len(causal)) + 1):
                r, c = 64 + 32 * (j // 4), j % 4
                mm = pe.matmul(bank[r:r + W, c * P:(c + 1) * P], self.Vst[q][:, j, :], self.PW[:, j, 0, :],
                               start=True, stop=j == 0)
                if j > 0:
                    mm = pe.matmul(bank[r:r + W, c * P:(c + 1) * P], self.Vst[q][:, j - 1, :], self.PW[:, j - 1, 1, :],
                                   start=False, stop=True)
        return mm

    def pe_head(self, q, more, copied, probs):
        pe, LAG = self.pe, 3
        N = self.pe_score_pieces()
        num, den = (4, 3) if self.window else (3, 2)
        pe.wait_ge(self.s["Mt_ready"], self.pc["Mt_ready"].next())
        for n in range(N):
            self.pe_probs_piece(q, n)
            if more:
                if n == 0:
                    pe.wait_ge(self.s["Q_copied"], copied)
                    pe.wait_ge(self.s["K_copied"], copied)
                for m in range(n * num // den, min((n + 1) * num // den, N)):
                    self.pe_scores_piece(1 - q, m)
            if n == LAG:
                pe.wait_ge(self.s["PV_taken"], self.pc["PV_taken"].next())
            if n >= LAG:
                self.pe_values_piece(q, n - LAG)
        if more:
            self.pe_maxT()
        for n in range(N - LAG, N):
            if n == N - 2:
                pe.wait_ge(self.s["P_ready"], probs)
            mm = self.pe_values_piece(q, n)
        mm.then_inc(self.s["PV_ready"], 1)

    def pe_output(self):
        pe = self.pe
        pe.wait_ge(self.s["PV_copied"], self.pc["PV_copied"].next())
        pe.sem_inc(self.s["apart"], 1)
        for c in range(4):
            mm = pe.transpose(self.ps[7].f32[:, c * P:c * P + self.OR], self.Orows[:, c * P:(c + 1) * P],
                              self.identf[0:self.OR, 0:self.OR])
        mm.then_inc(self.s["out_turned"], 1)


    def act_cursors(self, act):
        self.act = act
        self.ac = {n: Cursor(act, self.s[n]) for n in ("Q_turned", "ST_ready", "PV_ready")}

    def act_turn(self, q, v):
        self.act.wait_ge(self.s["Q_turned"], self.ac["Q_turned"].next())
        self.act.copy(self.QT[q][0:self.R, :], self.ps[0].bitcast_bf16[0:self.R, :])
        self.act.copy(self.Vst[q][:, :, :].rearrange("p c (o d) -> p c o d", o=1), v).then_inc(self.s["Q_copied"], 1)

    def act_output(self):
        self.act.wait_ge(self.s["PV_ready"], self.ac["PV_ready"].next())
        self.act.copy(self.Orows[:, :], self.ps[7].f32[0:self.OR, :]).then_inc(self.s["PV_copied"], 1)

    def act_exps(self):
        act = self.act
        n = 0
        for j, t0, tn in causal_probs():
            o = causal_block(j, t0)
            self.act.wait_ge(self.s["ST_ready"], self.ac["ST_ready"].next())
            act.activation(self.PT[:, o:o + tn, :], self.ps[5 + n % 2].f32[:, 0:tn * P], ACT.Exp)\
               .then_inc(self.s["P_ready"], 1)
            n += 1
        if self.window:
            for j2 in range(0, NT, 2):
                w = 4 if j2 + 2 < NT else 3
                self.act.wait_ge(self.s["ST_ready"], self.ac["ST_ready"].next())
                act.activation(self.PW[:, j2:j2 + 2, :, :].rearrange("p a e t -> p (a e) t")[:, 0:w, :],
                               self.ps[5 + n % 2].f32[:, 0:w * P], ACT.Exp).then_inc(self.s["P_ready"], 1)
                n += 1


    def dve_cursors(self, dve):
        self.dve = dve
        self.dc = {n: Cursor(dve, self.s[n]) for n in ("S_ready", "S_taken", "maxT_ready", "K_turned", "out_turned")}
        self.own = Cursor(dve, self.s["own_dve"])
        dve.sem_inc(self.s["Q_copied"], 1)
        dve.sem_inc(self.s["K_copied"], 1)
        dve.sem_inc(self.s["S_taken"], 2)
        dve.sem_inc(self.s["P_ready"], 2)
        dve.memset(self.ps[7].f32[:, :], 0.0).then_inc(self.s["PV_taken"], 1)
        self.dc["S_taken"].n += 2

    OWN_HEAD = 5

    def dve_maxima(self):
        dve, own = self.dve, self.own
        n = 0
        for i, k0, kn, part in causal_scores():
            self.dve.wait_ge(self.s["S_ready"], self.dc["S_ready"].next())
            ins = dve.tensor_reduce(self.mp[:, part, 0, i:i + 1], self.ps[3 + n % 2].f32[:, 0:kn * P], AX, ALU.max)
            ins.then_inc(self.s["S_taken"], 1)
            n += 1
        if self.window:
            for i2 in range(0, NT, 2):
                self.dve.wait_ge(self.s["S_ready"], self.dc["S_ready"].next())
                ins = dve.tensor_reduce(self.mp[:, 0, 1, i2:i2 + 2],
                                        self.ps[3 + n % 2].f32[:, :].rearrange("p (a s) -> p a s", a=2), AX, ALU.max)
                ins.then_inc(self.s["S_taken"], 1)
                n += 1
        self.dve.wait_ge(self.s["S_taken"], self.dc["S_taken"].next(n))
        dve.tensor_tensor(self.nm[:, :, :], self.mp[:, 0, :, :], self.mp[:, 1, :, :], ALU.max).then_inc(self.s["own_dve"], 1)
        dve.wait_ge(self.s["own_dve"], own.next())
        dve.tensor_scalar(self.mb[:, 0, :, :], self.nm[:, :, :], -1.0, None, ALU.mult).then_inc(self.s["own_dve"], 1)
        dve.wait_ge(self.s["own_dve"], own.next())
        dve.scalar_tensor_tensor(out=self.rem[:, :, :], in0=self.nm[:, :, :], scalar=-1.0,
                                 in1=self.mb[:, 0, :, :], op0=ALU.mult, op1=ALU.subtract).then_inc(self.s["own_dve"], 1)
        dve.wait_ge(self.s["own_dve"], own.next())
        dve.tensor_copy(self.mb[:, 1, :, :], self.rem[:, :, :]).then_inc(self.s["own_dve"], 1)
        dve.wait_ge(self.s["own_dve"], own.next())
        dve.sem_inc(self.s["max_split"], 1)

    def dve_turn(self, q):
        self.dve.wait_ge(self.s["K_turned"], self.dc["K_turned"].next())
        self.dve.tensor_copy(self.KT[q][0:self.R, :], self.ps[1].bitcast_bf16[0:self.R, :])\
            .then_inc(self.s["K_copied"], 1)

    def dve_maxT(self):
        self.dve.wait_ge(self.s["maxT_ready"], self.dc["maxT_ready"].next())
        src = self.ps[2].bitcast_bf16[0:self.MR, 0:P].rearrange("r (o t) -> r o t", o=1).broadcast_to([self.MR, NT, P])
        for n in range(self.nb):
            ins = self.dve.tensor_tensor(self.Mt[n][:, :, :], self.rowmask[n], src, ALU.mult)
        ins.then_inc(self.s["Mt_ready"], 1)

    def dve_output(self, outs):
        self.dve.wait_ge(self.s["out_turned"], self.dc["out_turned"].next())
        views = [self.ps[7].f32[:, :].rearrange("p (c n h w) -> p n h c w", c=4, n=2, h=2)[:, n] for n in range(self.nb)]
        rden = [self.rden[:, n, :, :].rearrange("p (h c) o -> p h c o", h=2) for n in range(self.nb)]
        for n in range(self.nb):
            ins = self.dve.reciprocal(rden[n], views[n][:, :, :, self.DV:self.DV + 1])
        ins.then_inc(self.s["own_dve"], 1)
        self.dve.wait_ge(self.s["own_dve"], self.own.next())
        for n in range(self.nb):
            ins = self.dve.tensor_tensor(outs(n).rearrange("p (h c) d -> p h c d", h=2), views[n][:, :, :, 0:self.DV],
                                         rden[n].broadcast_to([P, 2, 4, self.DV]), ALU.mult)
        ins.then_inc(self.s["PV_taken"], 1)


class Bank:

    def __init__(self, t):
        self.f32 = t
        self.bitcast_bf16 = t[:, :].bitcast(BF16)


def split3(own, eng, parts, rest, src):
    eng.tensor_copy(parts[0], src).then_inc(own.sem, 1)
    eng.wait_ge(own.sem, own.next())
    eng.tensor_tensor(rest, src, parts[0], ALU.subtract).then_inc(own.sem, 1)
    eng.wait_ge(own.sem, own.next())
    eng.tensor_copy(parts[1], rest).then_inc(own.sem, 1)
    eng.wait_ge(own.sem, own.next())
    eng.tensor_tensor(rest, rest, parts[1], ALU.subtract).then_inc(own.sem, 1)
    eng.wait_ge(own.sem, own.next())
    eng.tensor_copy(parts[2], rest).then_inc(own.sem, 1)
    eng.wait_ge(own.sem, own.next())


def attention_constants(pool, own, ident, identf, ones, rowmask, mask, nb):
    W = 64
    pool.memset(identf[:, :], 0.0).then_inc(own.sem, 1)
    pool.wait_ge(own.sem, own.next())
    pool.affine_select(out=identf[:, :], in_=identf[:, :], compare_op=ALU.not_equal,
                       fill=1.0, base=0, pattern=[[-1, P]], channel_multiplier=1).then_inc(own.sem, 1)
    pool.wait_ge(own.sem, own.next())
    pool.tensor_copy(ident[:, :], identf[:, :]).then_inc(own.sem, 1)
    pool.wait_ge(own.sem, own.next())
    pool.memset(mask[:, 0:6, :], 0.0).then_inc(own.sem, 1)
    pool.wait_ge(own.sem, own.next())
    pool.memset(mask[:, 6, :], FAR).then_inc(own.sem, 1)
    pool.wait_ge(own.sem, own.next())
    sel = [(0, 0, -1, 1), (1, 0, 1, -1), (4, -W, 1, -1), (3, -W, -1, 1), (5, 0, -1, 1), (5, W, 1, -1),
           (2, 0, 1, -1), (2, W, -1, 1)]
    for m, base, step, mult in sel:
        pool.affine_select(out=mask[:, m, :], in_=mask[:, m, :], compare_op=ALU.is_ge, fill=FAR,
                           base=base, pattern=[[step, P]], channel_multiplier=mult).then_inc(own.sem, 1)
        pool.wait_ge(own.sem, own.next())
    pool.memset(ones[:, :], 1.0).then_inc(own.sem, 1)
    pool.wait_ge(own.sem, own.next())
    for n in range(nb):
        pool.memset(rowmask[n][:, :, :], 0.0).then_inc(own.sem, 1)
        pool.wait_ge(own.sem, own.next())
        for part in range(2):
            pool.affine_select(out=rowmask[n][:, :, :], in_=rowmask[n][:, :, :], compare_op=ALU.not_equal,
                               fill=1.0, base=-(part * nb + n) * NT, pattern=[[-1, NT], [0, P]],
                               channel_multiplier=1).then_inc(own.sem, 1)
            pool.wait_ge(own.sem, own.next())


def ssd_stage(nc, x_in, x_out, w):
    H, N, HD, J = 64, 64, 8, 32
    DI = H * HD
    PAIRS = H // 2
    SCALE = float(N) ** -0.5
    EPS = 1e-6
    TWO_PI = 2.0 * np.pi
    HALF_PI = float(np.pi / 2)
    SIN_SCALE = 6.2831845
    ROUND = float(3 << 22)
    with ExitStack() as ctx:
        def sb(name, shape, dt=F32):
            return ctx.enter_context(nc.sbuf_tensor("s_" + name, shape, dt))

        xin = sb("xin", [P, NT, D])
        Z = sb("Z", [P, NT, DI])
        XS = sb("XS", [P, NT, DI])
        BC = sb("BC", [P, NT, 2, N])
        U = sb("U", [P, NT, DI])
        UE = sb("UE", [P, NT, DI])
        Y = sb("Y", [P, NT, DI])
        VST = Y[:, :, :].rearrange("p c (v h f j) -> p c v h f j", v=4, h=2, f=2)
        VT = sb("VT", [P, 4, T])
        RB = [sb(f"RB{i}", [P, T]) for i in range(2)]
        RC = [sb(f"RC{i}", [P, T]) for i in range(2)]
        xT = [RB[0], RB[1]]
        E = [sb(f"E{i}", [P, T]) for i in range(2)]
        dtr, absd = E[0][0:H, :], E[1][0:H, :]
        laT = E[0][0:H, :]
        dtT = sb("dtT", [H, T])
        LT = sb("LT", [H, T])
        LTb12 = sb("LTb12", [P, T], BF16)
        LTb3 = sb("LTb3", [H, T], BF16)
        tau = sb("tau", [H, T])
        cmask = sb("cmask", [H, T], BF16)
        ones = sb("ones", [H, 1])
        Ltok = sb("Ltok", [P, NT, H])
        nL = sb("nL", [P, NT, H])
        eL = sb("eL", [P, NT, H])
        we = sb("we", [P, NT, H])
        Dm = sb("Dm", [H, PAIRS, NT])
        Dc = sb("Dc", [P, PAIRS, HD, NT])
        ang = sb("ang", [P, T])
        kk = sb("kk", [P, T])
        tB = sb("tB", [P, T])
        tC = sb("tC", [P, T])
        Btok = sb("Btok", [P, NT, P])
        S = sb("S", [P, 2, HD, NT])
        yi = sb("yi", [P, NT, 16])
        gT = [Btok[:, 0:4, :], Btok[:, 4:8, :]]
        Win = sb("Win", [P, KD, 2 * DI + 2 * N + H])
        Wout = sb("Wout", [P, DI // P, D])
        nw = sb("nw", [P, DI // P])
        ident = sb("ident", [P, P])
        identb = sb("identb", [P, P], BF16)
        maskb = sb("maskb", [P, 1, P], BF16)
        idp = sb("idp", [H, H + 8])
        idp2 = sb("idp2", [P, H + 8], BF16)
        sel127 = sb("sel127", [P, P])
        par = sb("par", [H, 2, N])
        maskp = sb("maskp", [H, PAIRS])
        freq = sb("freq", [H, J])
        F = sb("F", [H, 2, 2, J])
        sel = [[sb(f"sel{i}{h}", [P, P], BF16) for h in range(2)] for i in range(2)]
        dtb = sb("dtb", [H, 1])
        negA = sb("negA", [H, 1])
        Dbc = sb("Dbc", [P, H])
        bias = sb("bias", [P, 4, PAIRS + 2])
        sgn = sb("sgn", [P, 1])
        halfpi = sb("halfpi", [P, 1])
        zero = sb("zero", [P, 16])
        eps6 = sb("eps6", [P, 1])
        eps5 = sb("eps5", [P, 1])
        ss = sb("ss", [P, NT, 2])
        rs = sb("rs", [P, NT, 2])
        sg2 = sb("sg2", [P, NT])
        rg = sb("rg", [P, NT])
        stats = sb("stats", [P, NT, 6])
        mv = sb("mv", [P, NT, 2])
        rl = sb("rl", [P, NT, 1])
        ps = [ctx.enter_context(nc.psum_tensor(f"s_ps{i}", [P, 512], F32)) for i in range(8)]

        names = ("const cdma fold x_loaded stored batch_done transposed xT_copied z_ready z_taken xs_taken dtT_ready "
                 "dt_raw log_ready LT_ready tok_ready Ltok_ready Dm_ready Lend_ready Dc_ready we_arg we_ready "
                 "bc_sum bc_root bc_normed staged vT_ready vT_copied phi_ready angle_ready trig_ready "
                 "prodB_ready prodC_ready RB_ready RC_ready F_ready sel_ready turnB_ready Btok_ready U_ready S_ready "
                 "L_ready L_taken G_ready W_ready E_free Y_ready combined g_ready g_sum g_root gT_ready gT_copied "
                 "out_ready var std res own_dve own_act own_pool apart tri_free").split()
        s = stage_semaphores(nc, ctx, "s_", names)
        x_v = x_in.rearrange("(b c p) d -> b p c d", p=P, c=NT)
        o_v = x_out.rearrange("(b c p) d -> b p c d", p=P, c=NT)

        def cur(eng, *which):
            return [Cursor(eng, s[n]) for n in which]

        with nc.Block() as block:

            @block.sync
            def _(sp):
                loads = [(Win[:, :, :], w["W_in"].rearrange("(k p) n -> p k n", p=P)),
                         (Wout[:, :, :], w["W_out"].rearrange("(k p) n -> p k n", p=P)),
                         (nw[:, :], w["norm_w"]), (freq[:, :], w["freq"]),
                         (dtb[:, :], w["dt_bias"]), (negA[:, :], w["A_log"]),
                         (Dbc[:, :], w["D_param"].partition_broadcast(P)),
                         (bias[:, :, 0:PAIRS], w["bias"])]
                sp.wait_ge(s["const"], 1)
                for dst, src in loads:
                    sp.dma_start(dst, src).then_inc(s["cdma"], 16)
                res, stored = cur(sp, "res", "stored")
                with loop(sp, BATCH, (res, 1), (stored, 16)) as b:
                    sp.dma_start(xin[:, :, :], x_v[b]).then_inc(s["x_loaded"], 16)
                    sp.wait_ge(s["res"], res.next())
                    sp.sem_inc(s["apart"], 1)
                    sp.dma_start(o_v[b], xin[:, :, :]).then_inc(s["stored"], 16)
                    sp.wait_ge(s["stored"], stored.next(16))
                    sp.sem_inc(s["apart"], 1)

            @block.gpsimd
            def _(pool):
                own, apart = Cursor(pool, s["own_pool"]), s["apart"]
                pool.memset(ident[:, :], 0.0).then_inc(s["own_pool"], 1)
                pool.wait_ge(s["own_pool"], own.next())
                pool.affine_select(out=ident[:, :], in_=ident[:, :], compare_op=ALU.not_equal,
                                   fill=1.0, base=0, pattern=[[-1, P]], channel_multiplier=1).then_inc(s["own_pool"], 1)
                pool.wait_ge(s["own_pool"], own.next())
                pool.tensor_copy(identb[:, :], ident[:, :])
                pool.memset(maskb[:, :, :], 0.0).then_inc(s["own_pool"], 1)
                pool.wait_ge(s["own_pool"], own.next())
                pool.affine_select(out=maskb[:, 0, :], in_=maskb[:, 0, :], compare_op=ALU.is_ge,
                                   fill=NEG, base=0, pattern=[[1, P]], channel_multiplier=-1)\
                   .then_inc(s["own_pool"], 1)
                pool.wait_ge(s["own_pool"], own.next())
                pool.memset(idp[:, :], 0.0).then_inc(s["own_pool"], 1)
                pool.wait_ge(s["own_pool"], own.next())
                pool.affine_select(out=idp[:, :], in_=idp[:, :], compare_op=ALU.not_equal,
                                   fill=1.0, base=0, pattern=[[-1, H + 8]], channel_multiplier=1)\
                   .then_inc(s["own_pool"], 1)
                pool.wait_ge(s["own_pool"], own.next())
                pool.memset(sel127[:, :], 0.0).then_inc(s["own_pool"], 1)
                pool.wait_ge(s["own_pool"], own.next())
                pool.affine_select(out=sel127[:, :], in_=sel127[:, :], compare_op=ALU.not_equal,
                                   fill=1.0, base=-(P - 1), pattern=[[0, P]], channel_multiplier=1)\
                   .then_inc(s["own_pool"], 1)
                pool.wait_ge(s["own_pool"], own.next())
                pool.memset(idp2[:, :], 0.0).then_inc(s["own_pool"], 1)
                pool.wait_ge(s["own_pool"], own.next())
                for part in range(2):
                    pool.affine_select(out=idp2[:, :], in_=idp2[:, :], compare_op=ALU.not_equal, fill=1.0,
                                       base=-H * part, pattern=[[-1, H + 8]], channel_multiplier=1)\
                        .then_inc(s["own_pool"], 1)
                    pool.wait_ge(s["own_pool"], own.next())
                pool.memset(maskp[:, :], 1.0).then_inc(s["own_pool"], 1)
                pool.wait_ge(s["own_pool"], own.next())
                pool.affine_select(out=maskp[:, :], in_=maskp[:, :], compare_op=ALU.is_ge,
                                   fill=0.0, base=0, pattern=[[-2, PAIRS]], channel_multiplier=1)\
                   .then_inc(s["own_pool"], 1)
                pool.wait_ge(s["own_pool"], own.next())
                pool.affine_select(out=maskp[:, :], in_=maskp[:, :], compare_op=ALU.is_ge,
                                   fill=0.0, base=1, pattern=[[2, PAIRS]], channel_multiplier=-1)\
                   .then_inc(s["own_pool"], 1)
                pool.wait_ge(s["own_pool"], own.next())
                pool.memset(cmask[:, :], 1.0)
                pool.memset(ones[:, :], 1.0).then_inc(s["own_pool"], 1)
                pool.wait_ge(s["own_pool"], own.next())
                pool.memset(cmask[:, :].rearrange("h (c t) -> h c t", t=P)[:, :, 0:1], 0.0).then_inc(s["own_pool"], 1)
                pool.wait_ge(s["own_pool"], own.next())
                for q in range(4):
                    pool.memset(sgn[32 * q:32 * q + 32, :], (-1.0 if q % 2 == 0 else 1.0) * SIN_SCALE)\
                       .then_inc(s["own_pool"], 1)
                    pool.wait_ge(s["own_pool"], own.next())
                pool.memset(halfpi[:, :], HALF_PI)
                pool.memset(zero[:, :], 0.0)
                pool.memset(eps6[:, :], EPS)
                pool.memset(eps5[:, :], LN_EPS)
                pool.memset(Dc[:, :, :, 0:1], 0.0)
                pool.memset(S[:, :, :, :], 0.0)
                pool.memset(bias[:, :, :], 0.0).then_inc(s["own_pool"], 1)
                pool.wait_ge(s["own_pool"], own.next())
                pool.sem_inc(s["const"], 1)
                pool.wait_ge(s["cdma"], 8 * 16)
                pool.tensor_scalar(freq[:, :], freq[:, :], float(1.0 / TWO_PI), None, ALU.mult)\
                   .then_inc(s["own_pool"], 1)
                pool.wait_ge(s["own_pool"], own.next())
                norm, phi, pB, pC, comb, Fr, selr = cur(pool, "bc_normed", "phi_ready", "prodB_ready", "prodC_ready",
                                                        "combined", "F_ready", "sel_ready")

                def frequencies(p):
                    for hh in range(2):
                        ins = pool.tensor_tensor(F[:, hh, :, :],
                                                 freq[:, :].rearrange("h (o j) -> h o j", o=1).broadcast_to([H, 2, J]),
                                                 idp[:, bass.ds(2 * p + hh, 1)].rearrange("h (o j) -> h o j", o=1)
                                                 .broadcast_to([H, 2, J]), ALU.mult)
                    ins.then_inc(s["F_ready"], 1)

                def selectors(p, q):
                    for hh in range(2):
                        ins = pool.tensor_copy(sel[q][hh][:, :], idp2[:, bass.ds(2 * p + hh, 1)].broadcast_to([P, P]))
                    ins.then_inc(s["sel_ready"], 1)

                def rotate(q):
                    pool.wait_ge(s["prodB_ready"], pB.next())
                    pool.tensor_tensor(RB[q][:, :], RB[q][:, :], tB[:, :], ALU.add).then_inc(s["RB_ready"], 1)
                    pool.wait_ge(s["prodC_ready"], pC.next())
                    pool.tensor_tensor(RC[q][:, :], RC[q][:, :], tC[:, :], ALU.add).then_inc(s["RC_ready"], 1)

                with loop(pool, BATCH, (norm, 1), (phi, PAIRS + 2), (pB, PAIRS + 1), (pC, PAIRS + 1),
                          (comb, PAIRS), (Fr, PAIRS + 3), (selr, PAIRS + 1)) as b:
                    pool.wait_ge(s["bc_normed"], norm.next())
                    pool.sem_inc(apart, 1)
                    bcn = BC[:, :, :, :].rearrange("p c v (j f) -> p c v f j", f=2)
                    for v in range(2):
                        for hh in range(2):
                            for f in range(2):
                                pool.tensor_copy(VST[:, :, 2 * v, hh, f, :], bcn[:, :, v, f, :])
                                ins = pool.tensor_copy(VST[:, :, 2 * v + 1, hh, f, :], bcn[:, :, v, 1 - f, :])
                    ins.then_inc(s["staged"], 1)
                    frequencies(0)
                    pool.wait_ge(s["phi_ready"], phi.next())
                    pool.sem_inc(apart, 1)
                    frequencies(1)
                    pool.wait_ge(s["phi_ready"], phi.next())
                    pool.sem_inc(apart, 1)
                    frequencies(2)
                    selectors(0, 0)
                    rotate(0)
                    with loop(pool, PAIRS // 2, (phi, 2), (pB, 2), (pC, 2), (comb, 2)) as p2:
                        for q in range(2):
                            p = p2 * 2 + q
                            rotate(1 - q)
                            pool.wait_ge(s["phi_ready"], phi.next())
                            frequencies(p + 3)
                            pool.wait_ge(s["combined"], comb.next())
                            pool.sem_inc(apart, 1)
                            selectors(p + 1, 1 - q)
                    pool.wait_ge(s["F_ready"], Fr.next(PAIRS + 3))
                    pool.sem_inc(apart, 1)
                    pool.wait_ge(s["sel_ready"], selr.next(PAIRS + 1))
                    pool.sem_inc(apart, 1)

            @block.tensor
            def _(pe):
                apart = s["apart"]
                (xl, trc, zt, xst, LTr, Ltr, Dmr, stg, vtc, Fr, selr, ang_, RBr, RCr, Btc, Sr, Lt, Wr, comb, gr, gTc,
                 ores) = cur(pe, "x_loaded", "xT_copied", "z_taken", "xs_taken", "LT_ready", "Ltok_ready", "Dm_ready",
                             "staged", "vT_copied", "F_ready", "sel_ready", "angle_ready", "RB_ready", "RC_ready",
                             "Btok_ready", "S_ready", "L_taken", "W_ready", "combined", "g_ready", "gT_copied", "var")
                pe.wait_ge(s["const"], 1)
                pe.wait_ge(s["cdma"], 8 * 16)

                def phase():
                    pe.wait_ge(s["F_ready"], Fr.next())
                    for h in range(2):
                        mm = pe.matmul(ps[h][:, :], F[:, :, :, :], tau[:, h * 512:(h + 1) * 512],
                                       start=True, stop=True)
                    mm.then_inc(s["phi_ready"], 1)

                def decays(hh, h, q):
                    pe.wait_ge(s["L_taken"], Lt.next())
                    pe.matmul(ps[3 + h][:, :], sel[q][hh][:, :], LTb12[:, h * 512:(h + 1) * 512],
                              start=True, stop=False)
                    pe.matmul(ps[3 + h][:, :], sel[q][hh][0:H, :], LTb3[:, h * 512:(h + 1) * 512],
                              start=False, stop=False)
                    pe.matmul(ps[3 + h][:, :], identb[:, :], maskb[:, :, :].broadcast_to([P, 4, P]),
                              start=False, stop=True).then_inc(s["L_ready"], 1)

                def scores(hh, h, q):
                    pe.wait_ge(s["W_ready"], Wr.next())
                    for c in range(4 * h, 4 * h + 4):
                        r = slice(hh * N, hh * N + N)
                        mm = pe.matmul(ps[5 + h][:, (c % 4) * P:(c % 4 + 1) * P],
                                       RB[q][r, c * P:(c + 1) * P], RC[q][r, c * P:(c + 1) * P],
                                       start=True, stop=True)
                    mm.then_inc(s["G_ready"], 1)

                with loop(pe, BATCH, (xl, 16), (trc, 4), (zt, 8), (xst, 8), (LTr, 1), (Ltr, 1), (Dmr, 1), (stg, 1),
                          (vtc, 8), (Fr, PAIRS + 3), (selr, PAIRS + 1), (ang_, PAIRS + 2), (RBr, PAIRS + 1),
                          (RCr, PAIRS + 1), (Btc, 2 * PAIRS), (Sr, PAIRS), (Lt, 4 * PAIRS), (Wr, 4 * PAIRS),
                          (comb, PAIRS), (gr, 1), (gTc, 8), (ores, 1)) as b:
                    pe.wait_ge(s["x_loaded"], xl.next(16))
                    for j in range(4):
                        k, h = j // 2, j % 2
                        for c in range(4):
                            mm = pe.transpose(ps[j][:, c * P:(c + 1) * P], xin[:, h * 4 + c, k * P:(k + 1) * P],
                                              ident[:, :])
                        mm.then_inc(s["transposed"], 1)
                    pe.wait_ge(s["xT_copied"], trc.next(4))
                    for c in range(NT):
                        o = 4 * (1 - c % 2)
                        if c >= 2:
                            pe.wait_ge(s["z_taken"], zt.next())
                            pe.wait_ge(s["xs_taken"], xst.next())
                        for bank, lo, hi in ((0, 0, DI), (1, DI, 2 * DI), (2, 2 * DI, 2 * DI + 2 * N)):
                            for k in range(KD):
                                mm = pe.matmul(ps[o + bank][:, 0:hi - lo], xT[k][:, c * P:(c + 1) * P],
                                               Win[:, k, lo:hi], start=(k == 0), stop=(k == KD - 1))
                        mm.then_inc(s["z_ready"], 1)
                    for h in range(2):
                        for k in range(KD):
                            mm = pe.matmul(ps[3 + 4 * h][0:H, :], Win[:, k, 2 * DI + 2 * N:],
                                           xT[k][:, h * 512:(h + 1) * 512], start=(k == 0), stop=(k == KD - 1))
                    mm.then_inc(s["dtT_ready"], 1)
                    pe.wait_ge(s["z_taken"], zt.next(2))
                    pe.wait_ge(s["xs_taken"], xst.next(2))
                    pe.wait_ge(s["LT_ready"], LTr.next())
                    pe.sem_inc(apart, 1)
                    for c in range(NT):
                        pe.transpose(ps[0][:, c * H:(c + 1) * H], LT[:, c * P:(c + 1) * P], ident[0:H, 0:H])
                        mm = pe.transpose(ps[1][:, c * H:(c + 1) * H], dtT[:, c * P:(c + 1) * P], ident[0:H, 0:H])
                    mm.then_inc(s["tok_ready"], 1)
                    pe.wait_ge(s["Ltok_ready"], Ltr.next())
                    pe.matmul(ps[2][:, :], sel127[:, :], Ltok[:, :, :], start=True, stop=True).then_inc(s["Lend_ready"], 1)
                    pe.wait_ge(s["Dm_ready"], Dmr.next())
                    pe.matmul(ps[3][:, 0:PAIRS * NT], par[:, :, :], Dm[:, :, :], start=True, stop=True)\
                      .then_inc(s["Dc_ready"], 1)
                    pe.wait_ge(s["staged"], stg.next())
                    pe.sem_inc(apart, 1)
                    for j in range(8):
                        v, h = j // 2, j % 2
                        if j >= 4:
                            pe.wait_ge(s["vT_copied"], vtc.next())
                        for c in range(4):
                            mm = pe.transpose(ps[4 + j % 4][:, c * P:(c + 1) * P],
                                              Y[:, h * 4 + c, v * P:(v + 1) * P], ident[:, :])
                        mm.then_inc(s["vT_ready"], 1)
                    pe.wait_ge(s["vT_copied"], vtc.next(4))
                    pe.matmul(ps[7][:, 0:P].rearrange("p (d c) -> p d c", c=NT)[:, :, 0], ident[:, :], zero[:, :],
                              start=True, stop=True)
                    phase()
                    pe.wait_ge(s["angle_ready"], ang_.next())
                    phase()
                    with loop(pe, PAIRS // 2, (Fr, 2), (selr, 2), (ang_, 2), (RBr, 2), (RCr, 2), (Btc, 4), (Sr, 2),
                              (Lt, 8), (Wr, 8), (comb, 2)) as p2:
                        for q in range(2):
                            pe.wait_ge(s["RB_ready"], RBr.next())
                            for h in range(2):
                                pe.wait_ge(s["Btok_ready"], Btc.next())
                                for c in range(4):
                                    mm = pe.transpose(ps[2][:, c * P:(c + 1) * P],
                                                      RB[q][:, (4 * h + c) * P:(4 * h + c + 1) * P], ident[:, :])
                                mm.then_inc(s["turnB_ready"], 1)
                            pe.wait_ge(s["sel_ready"], selr.next())
                            pe.wait_ge(s["RC_ready"], RCr.next())
                            for h in range(2):
                                decays(0, h, q)
                            for h in range(2):
                                scores(0, h, q)
                            pe.wait_ge(s["Btok_ready"], (b * PAIRS + p2 * 2 + q + 1) * 2 + 1)
                            pe.wait_ge(s["combined"], comb.next())
                            ub = ps[7][:, 0:P].rearrange("p (d c) -> p d c", c=NT)
                            for c in range(NT - 1):
                                mm = pe.matmul(ub[:, :, c + 1], Btok[:, c, :],
                                               UE[:, c, bass.ds((p2 * 2 + q) * 16, 16)], start=True, stop=True)
                            mm.then_inc(s["U_ready"], 1)
                            pe.wait_ge(s["angle_ready"], ang_.next())
                            phase()
                            for h in range(2):
                                decays(1, h, q)
                                scores(1, h, q)
                            pe.wait_ge(s["S_ready"], Sr.next())
                            for c in range(NT):
                                pe.matmul(ps[7][:, 256 + c * 16:256 + c * 16 + 16], RC[q][:, c * P:(c + 1) * P],
                                          S[:, :, :, c], start=True, stop=True)
                            pe.wait_ge(s["W_ready"], (b * PAIRS + p2 * 2 + q + 1) * 4 + 2)
                            for hh in range(2):
                                for c in range(NT):
                                    mm = pe.matmul(ps[7][:, 128 + c * 16 + hh * 8:128 + c * 16 + hh * 8 + 8],
                                                   E[hh][:, c * P:(c + 1) * P],
                                                   U[:, c, bass.ds((p2 * 2 + q) * 16 + hh * 8, 8)], start=True, stop=True)
                            mm.then_inc(s["Y_ready"], 1)
                    pe.wait_ge(s["angle_ready"], ang_.next())
                    pe.wait_ge(s["RB_ready"], RBr.next())
                    pe.wait_ge(s["RC_ready"], RCr.next())
                    pe.wait_ge(s["F_ready"], Fr.next())
                    pe.wait_ge(s["sel_ready"], selr.next())
                    pe.wait_ge(s["g_ready"], gr.next())
                    for c in range(NT):
                        for k in range(4):
                            mm = pe.transpose(ps[c % 2][:, k * P:(k + 1) * P], Y[:, c, k * P:(k + 1) * P], ident[:, :])
                        mm.then_inc(s["gT_ready"], 1)
                        pe.wait_ge(s["gT_copied"], gTc.next())
                        for k in range(4):
                            mm = pe.matmul(ps[4 + c // 2][:, (c % 2) * D:(c % 2 + 1) * D], gT[c % 2][:, k, :], Wout[:, k, :],
                                           start=(k == 0), stop=(k == 3))
                        if c % 2:
                            mm.then_inc(s["out_ready"], 1)
                    pe.wait_ge(s["var"], ores.next())

            @block.scalar
            def _(act):
                (tr, zr, absr, ltk, Dcr, wea, bcs, vt, anr, tB_, Lr, Yr, gr, gTr, var, efree) = cur(
                    act, "transposed", "z_ready", "dt_raw", "Ltok_ready", "Dc_ready", "we_arg", "bc_sum", "vT_ready",
                    "angle_ready", "turnB_ready", "L_ready", "Y_ready", "g_ready", "gT_ready", "var", "E_free")
                own = Cursor(act, s["own_act"])
                act.wait_ge(s["const"], 1)
                act.wait_ge(s["cdma"], 8 * 16)
                act.activation(negA[:, :], negA[:, :], ACT.Exp).then_inc(s["own_act"], 1)
                act.wait_ge(s["own_act"], own.next())
                act.activation(negA[:, :], negA[:, :], ACT.Copy, scale=-1.0).then_inc(s["own_act"], 1)
                act.wait_ge(s["own_act"], own.next())
                for k in range(4):
                    act.activation(Wout[:, k, :], Wout[:, k, :], ACT.Copy, scale=nw[:, k:k + 1])\
                       .then_inc(s["own_act"], 1)
                    act.wait_ge(s["own_act"], own.next())
                act.sem_inc(s["fold"], 1)

                def trig():
                    act.wait_ge(s["angle_ready"], anr.next())
                    act.activation(kk[:, :], ang[:, :], ACT.Abs).then_inc(s["own_act"], 1)
                    act.wait_ge(s["own_act"], own.next())
                    act.activation(kk[:, :], kk[:, :], ACT.Sin, bias=halfpi[:, 0:1], scale=-SIN_SCALE)
                    act.activation(ang[:, :], ang[:, :], ACT.Sin, scale=sgn[:, 0:1]).then_inc(s["trig_ready"], 1)

                with loop(act, BATCH, (tr, 4), (zr, 8), (absr, 1), (ltk, 1), (Dcr, 1), (wea, 1), (bcs, 1), (vt, 8),
                          (anr, PAIRS + 2), (tB_, 2 * PAIRS), (Lr, 4 * PAIRS), (Yr, PAIRS), (gr, 1), (gTr, 8),
                          (var, 1), (own, PAIRS + 5)) as b:
                    for j in range(4):
                        k, h = j // 2, j % 2
                        act.wait_ge(s["transposed"], tr.next())
                        act.copy(xT[k][:, h * 512:(h + 1) * 512], ps[j][:, :]).then_inc(s["xT_copied"], 1)
                    for c in range(NT):
                        act.wait_ge(s["z_ready"], zr.next())
                        act.activation(Z[:, c, :], ps[4 * (1 - c % 2)][:, :], ACT.Silu).then_inc(s["z_taken"], 1)
                    act.wait_ge(s["dt_raw"], absr.next())
                    act.activation(absd, dtr, ACT.Abs).then_inc(s["own_act"], 1)
                    act.wait_ge(s["own_act"], own.next())
                    act.activation(absd, absd, ACT.Exp, scale=-1.0).then_inc(s["own_act"], 1)
                    act.wait_ge(s["own_act"], own.next())
                    act.activation(absd, absd, ACT.Ln, bias=1.0).then_inc(s["log_ready"], 1)
                    act.wait_ge(s["Ltok_ready"], ltk.next())
                    act.activation(eL[:, :, :], Ltok[:, :, :], ACT.Exp)
                    act.wait_ge(s["Dc_ready"], Dcr.next())
                    act.activation(Dc[:, :, :, 1:NT].rearrange("p a d c -> p a d c"),
                                   ps[3][:, 0:PAIRS * NT].rearrange("p (a o c) -> p a o c", o=1, c=NT)[:, :, :, 1:NT]
                                   .broadcast_to([P, PAIRS, HD, NT - 1]), ACT.Exp)
                    act.wait_ge(s["we_arg"], wea.next())
                    act.activation(we[:, :, :], we[:, :, :], ACT.Exp).then_inc(s["we_ready"], 1)
                    act.wait_ge(s["bc_sum"], bcs.next())
                    act.activation(rs[:, :, :], ss[:, :, :], ACT.Sqrt, bias=eps6[:, 0:1], scale=1.0 / N)\
                       .then_inc(s["bc_root"], 1)
                    for j in range(8):
                        v, h = j // 2, j % 2
                        act.wait_ge(s["vT_ready"], vt.next())
                        act.copy(VT[:, v, h * 512:(h + 1) * 512], ps[4 + j % 4][:, :]).then_inc(s["vT_copied"], 1)
                    trig()
                    trig()
                    with loop(act, PAIRS // 2, (anr, 2), (tB_, 4), (Lr, 8), (Yr, 2), (own, 2)) as p2:
                        for q in range(2):
                            for h in range(2):
                                act.wait_ge(s["turnB_ready"], tB_.next())
                                act.copy(Btok[:, 4 * h:4 * h + 4, :], ps[2][:, :]).then_inc(s["Btok_ready"], 1)
                            for hh in range(2):
                                for h in range(2):
                                    act.wait_ge(s["L_ready"], Lr.next())
                                    for c in range(4 * h, 4 * h + 4):
                                        ins = act.activation(E[hh][:, c * P:(c + 1) * P],
                                                             ps[3 + h][:, (c % 4) * P:(c % 4 + 1) * P], ACT.Exp,
                                                             bias=nL[:, c, bass.ds((p2 * 2 + q) * 2 + hh, 1)])
                                    ins.then_inc(s["L_taken"], 1)
                            trig()
                            act.wait_ge(s["Y_ready"], Yr.next())
                    act.wait_ge(s["g_ready"], gr.next())
                    for c in range(NT):
                        ins = act.activation(U[:, c, :], Y[:, c, :], ACT.Square, accum_out=sg2[:, c:c + 1])
                    ins.then_inc(s["own_act"], 1)
                    act.wait_ge(s["own_act"], own.next())
                    act.activation(rg[:, :], sg2[:, :], ACT.Sqrt, bias=eps6[:, 0:1], scale=1.0 / DI)\
                       .then_inc(s["g_root"], 1)
                    for c in range(NT):
                        act.wait_ge(s["gT_ready"], gTr.next())
                        act.copy(gT[c % 2][:, :, :], ps[c % 2][:, :].rearrange("p (k t) -> p k t", k=4))\
                           .then_inc(s["gT_copied"], 1)
                    act.wait_ge(s["var"], var.next())
                    act.activation(rl[:, :, :], mv[:, :, 1:2], ACT.Sqrt, bias=eps5[:, 0:1]).then_inc(s["std"], 1)

            @block.vector
            def _(dve):
                own, apart = Cursor(dve, s["own_dve"]), s["apart"]
                (xl, zr, dtr_, logr, tokr, Lendr, wer, bcr, phi, trg, Ur, Lk, Gr, Yr, groot, outr, std, RCr, xst, prod) = cur(
                    dve, "x_loaded", "z_ready", "dtT_ready", "log_ready", "tok_ready", "Lend_ready", "we_ready", "bc_root",
                    "phi_ready", "trig_ready", "U_ready", "L_taken", "G_ready", "Y_ready", "g_root", "out_ready",
                    "std", "RC_ready", "xs_taken", "prodC_ready")
                dve.wait_ge(s["const"], 1)
                dve.wait_ge(s["cdma"], 8 * 16)
                dve.wait_ge(s["fold"], 1)
                for hh in range(2):
                    dve.tensor_reduce(par[:, hh, 0:1], idp[:, hh:H:2], AX, ALU.add).then_inc(s["own_dve"], 1)
                    dve.wait_ge(s["own_dve"], own.next())
                dve.tensor_copy(par[:, :, 1:N], par[:, :, 0:1].broadcast_to([H, 2, N - 1])).then_inc(s["own_dve"], 1)
                dve.wait_ge(s["own_dve"], own.next())
                dve.sem_inc(s["L_taken"], 2)
                dve.sem_inc(s["W_ready"], 2)
                dve.sem_inc(s["Btok_ready"], 1)
                dve.sem_inc(s["combined"], 1)
                Lk.n += 2

                def angles():
                    dve.wait_ge(s["phi_ready"], phi.next())
                    for h in range(2):
                        ins = dve.tensor_scalar(kk[:, h * 512:(h + 1) * 512], ps[h][:, :], ROUND, ROUND,
                                                ALU.add, ALU.subtract)
                    ins.then_inc(s["own_dve"], 1)
                    dve.wait_ge(s["own_dve"], own.next())
                    for h in range(2):
                        ins = dve.tensor_tensor(ang[:, h * 512:(h + 1) * 512], ps[h][:, :],
                                                kk[:, h * 512:(h + 1) * 512], ALU.subtract)
                    ins.then_inc(s["angle_ready"], 1)

                def products(p, q):
                    dve.wait_ge(s["trig_ready"], trg.next())
                    for v, R, tmp, name in ((0, RB, tB, "prodB_ready"), (2, RC, tC, "prodC_ready")):
                        dve.scalar_tensor_tensor(out=R[q][:, :], in0=VT[:, v, :], scalar=bias[:, v, bass.ds(p, 1)],
                                                 in1=kk[:, :], op0=ALU.add, op1=ALU.mult)
                        dve.scalar_tensor_tensor(out=tmp[:, :], in0=VT[:, v + 1, :],
                                                 scalar=bias[:, v + 1, bass.ds(p, 1)],
                                                 in1=ang[:, :], op0=ALU.add, op1=ALU.mult).then_inc(s[name], 1)

                def weights(hh, h):
                    dve.wait_ge(s["L_taken"], Lk.next())
                    dve.wait_ge(s["G_ready"], Gr.next())
                    dve.tensor_tensor(E[hh][:, h * 512:(h + 1) * 512], E[hh][:, h * 512:(h + 1) * 512],
                                      ps[5 + h][:, :], ALU.mult).then_inc(s["W_ready"], 1)

                with loop(dve, BATCH, (xl, 16), (zr, 8), (dtr_, 1), (logr, 1), (tokr, 1), (Lendr, 1), (wer, 1),
                          (bcr, 1), (phi, PAIRS + 2), (trg, PAIRS + 2), (Ur, PAIRS), (Lk, 4 * PAIRS), (Gr, 4 * PAIRS),
                          (Yr, PAIRS), (groot, 1), (outr, 4), (std, 1), (RCr, PAIRS + 1), (prod, PAIRS + 1), (xst, 8), (own, 4 * PAIRS + 28)) as b:
                    dve.wait_ge(s["x_loaded"], xl.next(16))
                    for c in range(NT):
                        o = 4 * (1 - c % 2)
                        dve.wait_ge(s["z_ready"], zr.next())
                        dve.tensor_copy(XS[:, c, :], ps[o + 1][:, :])
                        dve.tensor_copy(BC[:, c, :, :], ps[o + 2][:, 0:2 * N].rearrange("p (v n) -> p v n", v=2))\
                           .then_inc(s["xs_taken"], 1)
                    dve.wait_ge(s["dtT_ready"], dtr_.next())
                    for h in range(2):
                        ins = dve.tensor_scalar(dtr[:, h * 512:(h + 1) * 512], ps[3 + 4 * h][0:H, :], dtb[:, 0:1], None,
                                                ALU.add)
                    ins.then_inc(s["dt_raw"], 1)
                    dve.wait_ge(s["xs_taken"], xst.next(8))
                    sqv = UE[:, 0:2, :].rearrange("p a (c n) -> p (a c) n", n=2 * N)
                    dve.tensor_tensor(sqv, BC[:, :, :, :].rearrange("p c v n -> p c (v n)"),
                                      BC[:, :, :, :].rearrange("p c v n -> p c (v n)"), ALU.mult)\
                       .then_inc(s["own_dve"], 1)
                    dve.wait_ge(s["own_dve"], own.next())
                    dve.tensor_reduce(ss[:, :, :].rearrange("p c v -> p (c v)"),
                                      sqv.rearrange("p c (v n) -> p (c v) n", n=N), AX, ALU.add).then_inc(s["bc_sum"], 1)
                    dve.wait_ge(s["log_ready"], logr.next())
                    dve.scalar_tensor_tensor(out=dtT[:, :], in0=dtr, scalar=0.0, in1=absd,
                                             op0=ALU.max, op1=ALU.add).then_inc(s["own_dve"], 1)
                    dve.wait_ge(s["own_dve"], own.next())
                    dve.tensor_scalar(laT, dtT[:, :], negA[:, 0:1], None, ALU.mult).then_inc(s["own_dve"], 1)
                    dve.wait_ge(s["own_dve"], own.next())
                    dve.tensor_tensor_scan(LT[:, :], cmask[:, :], laT, 0.0, ALU.mult, ALU.add).then_inc(s["own_dve"], 1)
                    dve.wait_ge(s["own_dve"], own.next())
                    split3(own, dve, (LTb12[0:H, :], LTb12[H:, :], LTb3[:, :]), laT, LT[:, :])
                    dve.tensor_tensor_scan(tau[:, :], ones[:, 0:1].broadcast_to([H, T]), dtT[:, :], 0.0,
                                           ALU.mult, ALU.add).then_inc(s["own_dve"], 1)
                    dve.wait_ge(s["own_dve"], own.next())
                    dve.sem_inc(s["LT_ready"], 1)
                    lend = LT[:, :].rearrange("h (o c t) -> h o c t", o=1, t=P)[:, :, 0:NT - 1, P - 1]
                    dve.memset(Dm[:, :, 0:1], 0.0).then_inc(s["own_dve"], 1)
                    dve.wait_ge(s["own_dve"], own.next())
                    dve.tensor_tensor(Dm[:, :, 1:NT], lend.broadcast_to([H, PAIRS, NT - 1]),
                                      maskp[:, :].rearrange("h (p o) -> h p o", o=1)
                                      .broadcast_to([H, PAIRS, NT - 1]), ALU.mult).then_inc(s["own_dve"], 1)
                    dve.wait_ge(s["own_dve"], own.next())
                    dve.sem_inc(s["Dm_ready"], 1)
                    dve.wait_ge(s["tok_ready"], tokr.next())
                    dve.tensor_copy(Ltok[:, :, :], ps[0][:, :].rearrange("p (c h) -> p c h", c=NT))\
                       .then_inc(s["own_dve"], 1)
                    dve.wait_ge(s["own_dve"], own.next())
                    dve.sem_inc(s["Ltok_ready"], 1)
                    dve.tensor_tensor(U[:, :, :].rearrange("p c (h d) -> p (c h) d", d=HD),
                                      XS[:, :, :].rearrange("p c (h d) -> p (c h) d", d=HD),
                                      ps[1][:, :].rearrange("p (a o) -> p a o", o=1)
                                      .broadcast_to([P, NT * H, HD]), ALU.mult).then_inc(s["own_dve"], 1)
                    dve.wait_ge(s["own_dve"], own.next())
                    dve.tensor_scalar(nL[:, :, :], Ltok[:, :, :], -1.0, None, ALU.mult).then_inc(s["own_dve"], 1)
                    dve.wait_ge(s["own_dve"], own.next())
                    dve.wait_ge(s["Lend_ready"], Lendr.next())
                    dve.tensor_tensor(we[:, :, :], ps[2][:, :].rearrange("p (c h) -> p c h", c=NT), Ltok[:, :, :],
                                      ALU.subtract).then_inc(s["we_arg"], 1)
                    dve.wait_ge(s["bc_root"], bcr.next())
                    dve.reciprocal(rs[:, :, :], rs[:, :, :]).then_inc(s["own_dve"], 1)
                    dve.wait_ge(s["own_dve"], own.next())
                    dve.tensor_tensor(BC[:, :, :, :].rearrange("p c v n -> p (c v) n"),
                                      BC[:, :, :, :].rearrange("p c v n -> p (c v) n"),
                                      rs[:, :, :].rearrange("p c (v o) -> p (c v) o", o=1)
                                      .broadcast_to([P, NT * 2, N]), ALU.mult).then_inc(s["own_dve"], 1)
                    dve.wait_ge(s["own_dve"], own.next())
                    dve.sem_inc(s["bc_normed"], 1)
                    dve.wait_ge(s["we_ready"], wer.next())
                    dve.tensor_tensor(UE[:, :, :].rearrange("p c (h d) -> p (c h) d", d=HD),
                                      U[:, :, :].rearrange("p c (h d) -> p (c h) d", d=HD),
                                      we[:, :, :].rearrange("p c (h o) -> p (c h) o", o=1)
                                      .broadcast_to([P, NT * H, HD]), ALU.mult).then_inc(s["own_dve"], 1)
                    dve.wait_ge(s["own_dve"], own.next())
                    angles()
                    products(0, 0)
                    dve.wait_ge(s["prodC_ready"], prod.next())
                    angles()
                    with loop(dve, PAIRS // 2, (phi, 2), (trg, 2), (Ur, 2), (Lk, 8), (Gr, 8), (Yr, 2), (RCr, 2), (prod, 2),
                              (own, 2 * 4)) as p2:
                        for q in range(2):
                            p = p2 * 2 + q
                            for h in range(2):
                                weights(0, h)
                            dve.wait_ge(s["U_ready"], Ur.next())
                            for hh in range(2):
                                r = slice(hh * N, hh * N + N)
                                dve.tensor_tensor_scan(
                           S[r, hh, :, :].rearrange("p d c -> p (d c)"),
                           Dc[r, bass.ds(p, 1), :, :].rearrange("p a d c -> p (a d c)"),
                           ps[7][r, hh * 64:hh * 64 + 64], 0.0, ALU.mult, ALU.add).then_inc(s["own_dve"], 1)
                                dve.wait_ge(s["own_dve"], own.next())
                            dve.sem_inc(s["S_ready"], 1)
                            dve.wait_ge(s["RC_ready"], RCr.next())
                            products(p + 1, 1 - q)
                            for h in range(2):
                                weights(1, h)
                            dve.wait_ge(s["prodC_ready"], prod.next())
                            angles()
                            dve.wait_ge(s["Y_ready"], Yr.next())
                            dve.tensor_tensor(
                       yi[:, :, :].rearrange("p c (h d) -> p c h d", d=HD),
                       ps[7][:, 256:384].rearrange("p (c h d) -> p c h d", c=NT, d=HD),
                       eL[:, :, bass.ds(2 * p, 2)].rearrange("p c (h o) -> p c h o", o=1)
                       .broadcast_to([P, NT, 2, HD]), ALU.mult).then_inc(s["own_dve"], 1)
                            dve.wait_ge(s["own_dve"], own.next())
                            dve.tensor_tensor(Y[:, :, bass.ds(p * 16, 16)],
                                              ps[7][:, 128:256].rearrange("p (c d) -> p c d", c=NT),
                                              yi[:, :, :], ALU.add).then_inc(s["combined"], 1)
                    dve.wait_ge(s["trig_ready"], trg.next())
                    dve.wait_ge(s["RC_ready"], RCr.next())
                    dve.tensor_tensor(XS[:, :, :].rearrange("p c (h d) -> p c h d", d=HD),
                                      XS[:, :, :].rearrange("p c (h d) -> p c h d", d=HD),
                                      Dbc[:, :].rearrange("p (o h q) -> p o h q", o=1, q=1)
                                      .broadcast_to([P, NT, H, HD]), ALU.mult).then_inc(s["own_dve"], 1)
                    dve.wait_ge(s["own_dve"], own.next())
                    dve.scalar_tensor_tensor(out=Y[:, :, :], in0=Y[:, :, :], scalar=SCALE, in1=XS[:, :, :],
                                             op0=ALU.mult, op1=ALU.add).then_inc(s["own_dve"], 1)
                    dve.wait_ge(s["own_dve"], own.next())
                    dve.tensor_tensor(Y[:, :, :], Y[:, :, :], Z[:, :, :], ALU.mult).then_inc(s["own_dve"], 1)
                    dve.wait_ge(s["own_dve"], own.next())
                    dve.sem_inc(s["g_ready"], 1)
                    dve.wait_ge(s["g_root"], groot.next())
                    dve.reciprocal(rg[:, :], rg[:, :]).then_inc(s["own_dve"], 1)
                    dve.wait_ge(s["own_dve"], own.next())
                    for c in range(NT):
                        if c % 2 == 0:
                            dve.wait_ge(s["out_ready"], outr.next())
                        ins = dve.scalar_tensor_tensor(out=xin[:, c, :], in0=ps[4 + c // 2][:, (c % 2) * D:(c % 2 + 1) * D],
                                                       scalar=rg[:, c:c + 1], in1=xin[:, c, :], op0=ALU.mult, op1=ALU.add)
                    ins.then_inc(s["own_dve"], 1)
                    dve.wait_ge(s["own_dve"], own.next())
                    for c in range(NT):
                        ins = dve.bn_stats(stats[:, c, :], xin[:, c, :])
                    ins.then_inc(s["own_dve"], 1)
                    dve.wait_ge(s["own_dve"], own.next())
                    dve.sem_inc(apart, 1)
                    for c in range(NT):
                        ins = dve.bn_aggr(mv[:, c, :], stats[:, c, :])
                    ins.then_inc(s["var"], 1)
                    dve.wait_ge(s["std"], std.next())
                    dve.reciprocal(rl[:, :, :], rl[:, :, :]).then_inc(s["own_dve"], 1)
                    dve.wait_ge(s["own_dve"], own.next())
                    dve.tensor_tensor(xin[:, :, :], xin[:, :, :], mv[:, :, 0:1].broadcast_to([P, NT, D]),
                                      ALU.subtract).then_inc(s["own_dve"], 1)
                    dve.wait_ge(s["own_dve"], own.next())
                    dve.tensor_tensor(xin[:, :, :], xin[:, :, :], rl[:, :, :].broadcast_to([P, NT, D]), ALU.mult)\
                       .then_inc(s["res"], 1)


def nsa_stage(nc, x_in, x_out, kv_rows, w):
    NH, KV, G, DH = 32, 8, 4, 8
    BLK = 16
    NB = T // BLK
    NJ = NB + 1
    DK = KV * DH
    QW = NH * DH
    SCALE = float(DH) ** -0.5
    W64 = KV * NB
    with ExitStack() as ctx:
        def sb(name, shape, dt=F32):
            return ctx.enter_context(nc.sbuf_tensor("n_" + name, shape, dt))

        ident = sb("ident", [P, P], BF16)
        identf = sb("identf", [P, P])
        ones = sb("ones", [4 * NT, P], BF16)
        rowmask = [sb(f"rowmask{n}", [4 * NT, NT, P], BF16) for n in range(2)]
        mask = sb("mask", [P, 7, P], BF16)
        ps = [Bank(ctx.enter_context(nc.psum_tensor(f"n_ps{i}", [P, 512], F32))) for i in range(8)]
        A = Attention(nc, ctx, "n_", P, 6 * DH, DH, True,
                      dict(ident=ident, identf=identf, ones=ones, rowmask=[m[:, :, :] for m in rowmask], mask=mask, ps=ps, heads=KV))
        xin = sb("xin", [P, NT, D])
        QKV = sb("QKV", [P, NT, QW + 2 * DK])
        GT = sb("GT", [P, NT, NH, 3])
        QTf = sb("QTf", [P, KD, T])
        Oc = sb("Oc", [P, NT, QW])
        Of = sb("Of", [P, NT, QW])
        Ow = sb("Ow", [P, NT, QW])
        xT = Oc[:, :, :].rearrange("p c d -> p (c d)").rearrange("p (k t) -> p k t", k=KD)
        OT = QTf
        ptf = A.PT[:, :, :].rearrange("p a t -> p (a t)")
        CS = ptf[:, 0:NT * G * NJ].rearrange("p (a j) -> p a j", j=NJ)
        PC = ptf[:, NT * G * NJ:2 * NT * G * NJ].rearrange("p (a j) -> p a j", j=NJ)
        rest = ptf[:, 0:NT * QW].rearrange("p (c d) -> p c d", d=QW)
        pwf = A.PW[:, :, :, :].rearrange("p a e t -> p (a e t)")
        KB = pwf[0:NB, 0:BLK * 2 * DK].rearrange("p (s n) -> p s n", s=BLK)
        kbT = sb("kbT", [P, 2, W64])
        hid = sb("hid", [P, 2, W64])
        CK = sb("CK", [P, KV, G, NJ])
        CV = sb("CV", [NJ, KV, DH])
        PCT = [sb(f"PCT{i}", [NJ, G, P]) for i in range(2)]
        imp = sb("imp", [P, NT, NJ])
        val = sb("val", [P, NT, NB])
        mr = sb("mr", [P, NT, NB])
        top = sb("top", [P, NT, 8])
        MS = sb("MS", [P, NT, KV, NB], BF16)
        Qp = [sb(f"Qp{i}", [P, NT, QW], BF16) for i in range(3)]
        Kp = [sb(f"Kp{i}", [P, NT, DK], BF16) for i in range(3)]
        cadd = sb("cadd", [P, NT, NJ])
        ownb = sb("ownb", [P, NT, NB])
        cs = sb("cs", [P, NT, 2, DH // 2])
        tmp = sb("tmp", [P, 2, NT, NH, DH // 2])
        KBh = tmp[0:NB, :, :, :, :].rearrange("j a c h e -> j (a c h e)").rearrange("j (a m) -> j a m", m=P)
        WN = QW + 2 * DK + 3 * NH
        Win = sb("Win", [P, KD, WN])
        Wo = sb("Wo", [P, KD, D])
        W1 = sb("W1", [P, 2, P])
        b1 = sb("b1", [P, 2])
        W2k = sb("W2k", [P, P])
        W2v = sb("W2v", [P, DH])
        b2k = sb("b2k", [P, 1])
        b2v = sb("b2v", [NB, DH])
        memk = sb("memk", [P, 2])
        pos = sb("pos", [P, 2, KV])
        fm = sb("fm", [P, 16])
        bg = sb("bg", [P, 3 * NH])
        cmx = sb("cmx", [P, NT * G, 1])
        rc = sb("rc", [P, NT * G, 1])
        m2 = sb("m2", [P, NT, 1])
        ri = sb("ri", [P, NT, 1])
        stats = sb("stats", [P, NT, 6])
        mv = sb("mv", [P, NT, 2])
        rl = sb("rl", [P, NT, 1])
        eps5 = sb("eps5", [P, 1])
        names = ("const cdma x_loaded transposed xT_copied tok_ready tok_taken kv_stored kv_loaded kv_grouped qT_ready qT_copied "
                 "kb_ready kb_taken hid_ready hid_done ck_ready ck_taken rows_ready "
                 "cs_ready cs_taken c_sub c_exp i_sub i_exp pt_ready pt_copied oc_ready oc_taken split "
                 "gate_raw gate_ready OT_ready OT_copied mixed out_ready out_taken var std res stored").split()
        s = stage_semaphores(nc, ctx, "n_", names)
        apart = A.s["apart"]
        x_v = x_in.rearrange("(b c p) d -> b p c d", p=P, c=NT)
        o_v = x_out.rearrange("(b c p) d -> b p c d", p=P, c=NT)
        NPIECE = len(causal_probs()) + NT // 2

        def cur(eng, *which):
            return [Cursor(eng, s[n]) for n in which]

        with nc.Block() as block:

            @block.sync
            def _(sp):
                loads = [(Win[:, :, 0:QW + 2 * DK], w["w_qkv"].rearrange("(k p) n -> p k n", p=P)),
                         (Win[:, :, QW + 2 * DK:], w["w_gate"].rearrange("(k p) n -> p k n", p=P)),
                         (Wo[:, :, :], w["w_out"].rearrange("(k p) n -> p k n", p=P)),
                         (W1[:, 0, :], w["k_cw1"]), (W1[:, 1, :], w["v_cw1"]), (b1[:, :], w["cb1"]),
                         (W2k[:, :], w["k_cw2"]), (W2v[:, :], w["v_cw2"]), (b2k[:, :], w["k_cb2"]),
                         (b2v[:, :], w["v_cb2"].partition_broadcast(NB)), (memk[:, :], w["mem_ck"]),
                         (CV[NB:NJ, :, :], w["mem_cv"]), (pos[:, :, :], w["pos"]),
                         (bg[:, :], w["b_gate"].partition_broadcast(P)), (cs[:, :, :, :], w["rope_cs"])]
                assert len(loads) == 15
                for dst, src in loads:
                    sp.dma_start(dst, src).then_inc(s["cdma"], 16)
                rows, stk, res, sto = cur(sp, "rows_ready", "kv_stored", "res", "stored")
                kb_free = cur(sp, "kb_taken")[0]
                with loop(sp, BATCH, (rows, 1), (stk, 16), (res, 1), (sto, 16)) as b:
                    sp.dma_start(xin[:, :, :], x_v[b]).then_inc(s["x_loaded"], 16)
                    sp.wait_ge(s["rows_ready"], rows.next())
                    sp.dma_start(kv_rows.rearrange("(c p) n -> p c n", p=P), QKV[:, :, QW:]).then_inc(s["kv_stored"], 16)
                    sp.wait_ge(s["kv_stored"], stk.next(16))
                    sp.dma_start(KB, kv_rows.rearrange("(j s) n -> j s n", s=BLK)).then_inc(s["kv_loaded"], 16)
                    sp.wait_ge(s["res"], res.next())
                    sp.sem_inc(apart, 1)
                    sp.dma_start(o_v[b], xin[:, :, :]).then_inc(s["stored"], 16)
                    sp.wait_ge(s["stored"], sto.next(16))
                    sp.sem_inc(apart, 1)

            @block.gpsimd
            def _(pool):
                own = Cursor(pool, A.s["own_pool"])
                attention_constants(pool, own, ident, identf, ones, rowmask, mask, 2)
                pool.memset(eps5[:, :], LN_EPS).then_inc(A.s["own_pool"], 1)
                pool.wait_ge(A.s["own_pool"], own.next())
                pool.memset(A.mp[:, :, :, :], -3e38).then_inc(A.s["own_pool"], 1)
                pool.wait_ge(A.s["own_pool"], own.next())
                pool.memset(A.V[:, :, :, DH:], 1.0).then_inc(A.s["own_pool"], 1)
                pool.wait_ge(A.s["own_pool"], own.next())
                pool.memset(cadd[:, :, :], 0.0).then_inc(A.s["own_pool"], 1)
                pool.wait_ge(A.s["own_pool"], own.next())
                pool.affine_select(out=cadd[:, :, 0:NB], in_=cadd[:, :, 0:NB], compare_op=ALU.is_ge, fill=NEG,
                                   base=-BLK, pattern=[[P, NT], [-BLK, NB]], channel_multiplier=1)\
                   .then_inc(A.s["own_pool"], 1)
                pool.wait_ge(A.s["own_pool"], own.next())
                pool.memset(ownb[:, :, :], 1.0).then_inc(A.s["own_pool"], 1)
                pool.wait_ge(A.s["own_pool"], own.next())
                pool.affine_select(out=ownb[:, :, :], in_=ownb[:, :, :], compare_op=ALU.is_ge, fill=0.0,
                                   base=0, pattern=[[P, NT], [-BLK, NB]], channel_multiplier=1)\
                   .then_inc(A.s["own_pool"], 1)
                pool.wait_ge(A.s["own_pool"], own.next())
                pool.affine_select(out=ownb[:, :, :], in_=ownb[:, :, :], compare_op=ALU.is_ge, fill=0.0,
                                   base=BLK - 1, pattern=[[-P, NT], [BLK, NB]], channel_multiplier=-1)\
                   .then_inc(A.s["own_pool"], 1)
                pool.wait_ge(A.s["own_pool"], own.next())
                pool.memset(fm[:, :], 1.0).then_inc(A.s["own_pool"], 1)
                pool.wait_ge(A.s["own_pool"], own.next())
                pool.affine_select(out=fm[:, :], in_=fm[:, :], compare_op=ALU.is_ge, fill=0.0,
                                   base=0, pattern=[[-DH, 16]], channel_multiplier=1).then_inc(A.s["own_pool"], 1)
                pool.wait_ge(A.s["own_pool"], own.next())
                pool.affine_select(out=fm[:, :], in_=fm[:, :], compare_op=ALU.is_ge, fill=0.0,
                                   base=DH - 1, pattern=[[DH, 16]], channel_multiplier=-1).then_inc(A.s["own_pool"], 1)
                pool.wait_ge(A.s["own_pool"], own.next())
                for q in range(2):
                    pool.memset(A.qst[q][:, :, 6 * DH:NB], 0.0).then_inc(A.s["own_pool"], 1)
                    pool.wait_ge(A.s["own_pool"], own.next())
                    pool.memset(A.kst[q][:, :, 6 * DH:NB], 0.0).then_inc(A.s["own_pool"], 1)
                    pool.wait_ge(A.s["own_pool"], own.next())
                    pool.tensor_copy(A.kst[q][:, :, NB:], ownb[:, :, :]).then_inc(A.s["own_pool"], 1)
                    pool.wait_ge(A.s["own_pool"], own.next())
                pool.memset(imp[:, :, :], -4000.0).then_inc(A.s["own_pool"], 1)
                pool.wait_ge(A.s["own_pool"], own.next())
                pool.sem_inc(s["const"], 1)
                split, tc = cur(pool, "split")[0], Cursor(pool, A.s["K_turned"])

                def stage(kv, g, q):
                    def qpart(x):
                        return x[:, :, bass.ds(kv * G * DH + g * DH, DH)].rearrange("p c (o d) -> p c o d", o=1)

                    def kpart(x):
                        return x[:, :, bass.ds(kv * DH, DH)].rearrange("p c (o d) -> p c o d", o=1)

                    qs = A.qst[q][:, :, 0:6 * DH].rearrange("p c (a d) -> p c a d", d=DH)
                    ks = A.kst[q][:, :, 0:6 * DH].rearrange("p c (a d) -> p c a d", d=DH)
                    for a in range(3):
                        pool.tensor_copy(qs[:, :, a:a + 1, :], qpart(Qp[a]))
                    for a in range(2):
                        pool.tensor_copy(qs[:, :, 3 + a:4 + a, :], qpart(Qp[a]))
                    pool.tensor_copy(qs[:, :, 5:6, :], qpart(Qp[0]))
                    pool.tensor_copy(ks[:, :, 0:3, :], kpart(Kp[0]).broadcast_to([P, NT, 3, DH]))
                    pool.tensor_copy(ks[:, :, 3:5, :], kpart(Kp[1]).broadcast_to([P, NT, 2, DH]))
                    pool.tensor_copy(ks[:, :, 5:6, :], kpart(Kp[2]))
                    pool.tensor_copy(A.qst[q][:, :, NB:].rearrange("p c (o j) -> p c o j", o=1),
                                     MS[:, :, bass.ds(kv, 1), :]).then_inc(A.s["staged"], 1)

                with loop(pool, BATCH, (split, 1), (tc, NH)) as b:
                    pool.wait_ge(s["split"], split.next())
                    pool.sem_inc(apart, 1)
                    stage(0, 0, 0)
                    stage(0, 1, 1)

                    def group(kv, last):
                        for g in range(G):
                            pool.wait_ge(A.s["K_turned"], tc.next())
                            pool.sem_inc(apart, 1)
                            if g < G - 2:
                                stage(kv, g + 2, g % 2)
                            elif not last:
                                stage(kv + 1, g + 2 - G, g % 2)

                    with loop(pool, KV - 1, (tc, G)) as kv:
                        group(kv, False)
                    group(KV - 1, True)

            @block.tensor
            def _(pe):
                A.pe_cursors(pe)
                pc = A.pc
                (xl, trc, tokt, qTc, kvl, kbt, hidd, ckt, cst, cexp, ptc, oct_, mixed, OTc, outt) = cur(
                    pe, "x_loaded", "xT_copied", "tok_taken", "qT_copied", "kv_grouped", "kb_taken", "hid_done", "ck_taken",
                    "cs_taken", "c_exp", "pt_copied", "oc_taken", "mixed", "OT_copied", "out_taken")
                pe.wait_ge(s["const"], 1)
                pe.wait_ge(s["cdma"], 15 * 16)
                def turn(c):
                    pe.wait_ge(s["pt_copied"], ptc.next())
                    for g in range(G):
                        mm = pe.transpose(ps[2 + c % 2].f32[0:NJ, g * P:(g + 1) * P], PC[:, c * G + g, :], identf[:, :])
                    mm.then_inc(s["pt_ready"], 1)

                with loop(pe, BATCH, (xl, 16), (trc, 4), (tokt, 8), (qTc, 4), (kvl, 1), (kbt, 1), (hidd, 2), (ckt, 1),
                          (cst, 8 * KV), (cexp, KV), (ptc, 8 * KV), (oct_, KV), (mixed, 1), (OTc, 4), (outt, 4),
                          (pc["staged"], NH), (pc["Q_copied"], NH), (pc["K_copied"], NH), (pc["max_split"], NH),
                          (pc["Mt_ready"], NH), (pc["S_taken"], NPIECE * NH), (pc["P_ready"], NPIECE * NH),
                          (pc["PV_taken"], NH), (pc["PV_copied"], NH)) as b:
                    pe.wait_ge(s["x_loaded"], xl.next(16))
                    for j in range(4):
                        k, h = j // 2, j % 2
                        for c in range(4):
                            mm = pe.transpose(ps[j].f32[:, c * P:(c + 1) * P], xin[:, h * 4 + c, k * P:(k + 1) * P],
                                              identf[:, :])
                        mm.then_inc(s["transposed"], 1)
                    pe.wait_ge(s["xT_copied"], trc.next(4))
                    for c in range(NT):
                        if c >= 2:
                            pe.wait_ge(s["tok_taken"], tokt.next())
                        for k in range(KD):
                            mm = pe.matmul(ps[4 + c % 2].f32[:, 0:WN], xT[:, k, c * P:(c + 1) * P], Win[:, k, :],
                                           start=(k == 0), stop=(k == KD - 1))
                        mm.then_inc(s["tok_ready"], 1)
                    pe.wait_ge(s["tok_taken"], tokt.next(2))
                    for j in range(4):
                        k, h = j // 2, j % 2
                        for c in range(4):
                            mm = pe.transpose(ps[j].f32[:, c * P:(c + 1) * P], QKV[:, h * 4 + c, k * P:(k + 1) * P],
                                              identf[:, :])
                        mm.then_inc(s["qT_ready"], 1)
                    pe.wait_ge(s["qT_copied"], qTc.next(4))
                    pe.wait_ge(s["kv_grouped"], kvl.next())
                    pe.sem_inc(apart, 1)
                    for v in range(2):
                        for h in range(KV):
                            mm = pe.transpose(ps[v].f32[:, h * NB:(h + 1) * NB], KBh[:, v * KV + h, :],
                                              identf[0:NB, 0:NB])
                    mm.then_inc(s["kb_ready"], 1)
                    pe.wait_ge(s["kb_taken"], kbt.next())
                    for v in range(2):
                        pe.matmul(ps[2 + v].f32[:, :], W1[:, v, :], kbT[:, v, :], start=True, stop=True)\
                          .then_inc(s["hid_ready"], 1)
                    pe.wait_ge(s["hid_done"], hidd.next(2))
                    pe.matmul(ps[0].f32[:, :], W2k[:, :], hid[:, 0, :], start=True, stop=True)
                    for h in range(KV):
                        mm = pe.matmul(ps[1].f32[0:NB, h * DH:(h + 1) * DH], hid[:, 1, h * NB:(h + 1) * NB], W2v[:, :],
                                       start=True, stop=True)
                    mm.then_inc(s["ck_ready"], 1)
                    pe.wait_ge(s["ck_taken"], ckt.next())
                    pe.sem_inc(apart, 1)
                    for hk in range(2):
                        with loop(pe, G, (cst, 8), (cexp, 1), (ptc, 8), (oct_, 1)) as hm:
                            for c in range(NT):
                                pe.wait_ge(s["cs_taken"], cst.next())
                                pe.matmul(ps[c % 2].f32[:, 0:G * NJ], QTf[:, hk, c * P:(c + 1) * P],
                                          CK[:, bass.ds(hk * G + hm, 1), :, :],
                                          start=True, stop=True).then_inc(s["cs_ready"], 1)
                            pe.wait_ge(s["c_exp"], cexp.next())
                            pe.sem_inc(apart, 1)
                            pe.wait_ge(s["oc_taken"], oct_.next())
                            pe.sem_inc(apart, 1)
                            turn(0)
                            for c in range(NT):
                                if c < NT - 1:
                                    turn(c + 1)
                                pe.wait_ge(s["pt_copied"], ((b * KV + hk * G + hm) * 8 + c + 1) + 2)
                                for g in range(G):
                                    o = (c * G + g) * DH
                                    mm = pe.matmul(ps[4].f32[:, o:o + DH], PCT[c % 2][:, g, :],
                                                   CV[:, bass.ds(hk * G + hm, 1), :], start=True, stop=True)
                            mm.then_inc(s["oc_ready"], 1)
                    pe.wait_ge(s["oc_taken"], (b + 1) * KV + 1)
                    A.pe_turn(0)
                    A.pe_turn(1)
                    A.pe_scores(0, b * NH + 2)
                    A.pe_maxT()

                    def group(kv, last):
                        for g in range(G):
                            q = g % 2
                            n = kv * G + g
                            more = not (last and g == G - 1)
                            A.pe_head(q, more, b * NH + n + 3, (b * NH + n + 1) * NPIECE + 2)
                            if not (last and g >= G - 2):
                                A.pe_turn(q)
                            A.pe_output()

                    with loop(pe, KV - 1, (pc["staged"], G), (pc["Q_copied"], G), (pc["K_copied"], G), (pc["max_split"], G),
                              (pc["Mt_ready"], G), (pc["S_taken"], NPIECE * G), (pc["P_ready"], NPIECE * G),
                              (pc["PV_taken"], G), (pc["PV_copied"], G)) as kv:
                        group(kv, False)
                    group(KV - 1, True)
                    pe.wait_ge(s["mixed"], mixed.next())
                    for j in range(4):
                        k, h = j // 2, j % 2
                        for c in range(4):
                            mm = pe.transpose(ps[j].f32[:, c * P:(c + 1) * P], Oc[:, h * 4 + c, k * P:(k + 1) * P],
                                              identf[:, :])
                        mm.then_inc(s["OT_ready"], 1)
                    pe.wait_ge(s["OT_copied"], OTc.next(4))
                    for c in range(NT):
                        for k in range(KD):
                            mm = pe.matmul(ps[4 + c // 2].f32[:, (c % 2) * D:(c % 2 + 1) * D],
                                           OT[:, k, c * P:(c + 1) * P], Wo[:, k, :], start=(k == 0), stop=(k == KD - 1))
                        if c % 2:
                            mm.then_inc(s["out_ready"], 1)
                    pe.wait_ge(s["out_taken"], outt.next(4))

            @block.scalar
            def _(act):
                A.act_cursors(act)
                ac = A.ac
                tr, qTr, hidr, csub, isub, ptr, graw, OTr, var = cur(
                    act, "transposed", "qT_ready", "hid_ready", "c_sub", "i_sub", "pt_ready", "gate_raw", "OT_ready", "var")
                act.wait_ge(s["const"], 1)
                act.wait_ge(s["cdma"], 15 * 16)
                act.sem_inc(s["pt_copied"], 2)
                with loop(act, BATCH, (tr, 4), (qTr, 4), (hidr, 2), (csub, KV), (isub, KV), (ptr, 8 * KV), (graw, 1),
                          (OTr, 4), (var, 1), (ac["Q_turned"], NH), (ac["ST_ready"], NPIECE * NH),
                          (ac["PV_ready"], NH)) as b:
                    for j in range(4):
                        k, h = j // 2, j % 2
                        act.wait_ge(s["transposed"], tr.next())
                        act.copy(xT[:, k, h * 512:(h + 1) * 512], ps[j].f32[:, :]).then_inc(s["xT_copied"], 1)
                    act.wait_ge(s["gate_raw"], graw.next())
                    act.activation(GT[:, :, :, :], GT[:, :, :, :], ACT.Sigmoid).then_inc(s["gate_ready"], 1)
                    for j in range(4):
                        k, h = j // 2, j % 2
                        act.wait_ge(s["qT_ready"], qTr.next())
                        act.copy(QTf[:, k, h * 512:(h + 1) * 512], ps[j].f32[:, :]).then_inc(s["qT_copied"], 1)
                    for v in range(2):
                        act.wait_ge(s["hid_ready"], hidr.next())
                        act.activation(hid[:, v, :], ps[2 + v].f32[:, :], ACT.Relu, bias=b1[:, v:v + 1])\
                           .then_inc(s["hid_done"], 1)
                    with loop(act, KV, (csub, 1), (isub, 1), (ptr, 8)):
                        act.wait_ge(s["c_sub"], csub.next())
                        act.activation(PC, PC, ACT.Exp).then_inc(s["c_exp"], 1)
                        for c in range(NT):
                            if c == 1:
                                act.wait_ge(s["i_sub"], isub.next())
                                act.activation(imp[:, :, :], imp[:, :, :], ACT.Exp, scale=0.25).then_inc(s["i_exp"], 1)
                            act.wait_ge(s["pt_ready"], ptr.next())
                            act.copy(PCT[c % 2][:, :, :], ps[2 + c % 2].f32[0:NJ, :].rearrange("p (g t) -> p g t", g=G))\
                               .then_inc(s["pt_copied"], 1)
                    A.act_turn(0, A.V[:, :, 0:1, :])
                    A.act_turn(1, A.V[:, :, 0:1, :])

                    def group(kv, last):
                        for g in range(G):
                            A.act_exps()
                            A.act_output()
                            if g < G - 2:
                                A.act_turn(g % 2, A.V[:, :, bass.ds(kv, 1), :])
                            elif not last:
                                A.act_turn(g % 2, A.V[:, :, bass.ds(kv + 1, 1), :])

                    with loop(act, KV - 1, (ac["Q_turned"], G), (ac["ST_ready"], NPIECE * G), (ac["PV_ready"], G)) as kv:
                        group(kv, False)
                    group(KV - 1, True)
                    for j in range(4):
                        k, h = j // 2, j % 2
                        act.wait_ge(s["OT_ready"], OTr.next())
                        act.copy(OT[:, k, h * 512:(h + 1) * 512], ps[j].f32[:, :]).then_inc(s["OT_copied"], 1)
                    act.wait_ge(s["var"], var.next())
                    act.activation(rl[:, :, :], mv[:, :, 1:2], ACT.Sqrt, bias=eps5[:, 0:1]).then_inc(s["std"], 1)

            @block.vector
            def _(dve):
                A.dve_cursors(dve)
                dc, own = A.dc, A.own
                xl, tokr, qTr, kvl, kbr, ckr, csr, cstk, cexp, iexp, ocr, gr, outr, std = cur(
                    dve, "x_loaded", "tok_ready", "qT_copied", "kv_loaded", "kb_ready", "ck_ready", "cs_ready", "cs_taken",
                    "c_exp", "i_exp", "oc_ready", "gate_ready", "out_ready", "std")
                dve.wait_ge(s["const"], 1)
                dve.wait_ge(s["cdma"], 15 * 16)
                for h in range(KV):
                    ins = dve.tensor_scalar(CK[:, h, :, NB:NJ].rearrange("p g o -> p (g o)"),
                                            fm[:, (h % 4) * G:(h % 4 + 1) * G], memk[:, h // 4:h // 4 + 1], None, ALU.mult)
                ins.then_inc(A.s["own_dve"], 1)
                dve.wait_ge(A.s["own_dve"], own.next())
                dve.sem_inc(s["cs_taken"], 2)
                cstk.n += 2
                dve.sem_inc(s["oc_taken"], 1)
                with loop(dve, BATCH, (xl, 16), (tokr, 8), (kvl, 16), (kbr, 1), (ckr, 1), (csr, 8 * KV),
                          (cstk, 8 * KV), (cexp, KV), (iexp, KV), (ocr, KV), (gr, 1), (outr, 4), (std, 1),
                          (dc["S_ready"], NPIECE * NH), (dc["S_taken"], NPIECE * NH), (dc["maxT_ready"], NH),
                          (dc["K_turned"], NH), (dc["out_turned"], NH), (own, A.OWN_HEAD * NH + 25 + 16 * KV)) as b:
                    dve.wait_ge(s["x_loaded"], xl.next(16))
                    for c in range(NT):
                        dve.wait_ge(s["tok_ready"], tokr.next())
                        bank = ps[4 + c % 2].f32
                        dve.tensor_scalar(QKV[:, c, 0:QW], bank[:, 0:QW], SCALE, None, ALU.mult)
                        dve.tensor_copy(QKV[:, c, QW:], bank[:, QW:QW + 2 * DK])
                        ins = dve.tensor_tensor(GT[:, c, :, :].rearrange("p h e -> p (h e)"), bank[:, QW + 2 * DK:WN],
                                                bg[:, :], ALU.add)
                        if c < NT - 1:
                            ins.then_inc(s["tok_taken"], 1)
                        else:
                            ins.then_inc(A.s["own_dve"], 1)
                            dve.wait_ge(A.s["own_dve"], own.next())
                    dve.sem_inc(s["tok_taken"], 1)
                    dve.sem_inc(s["rows_ready"], 1)
                    dve.sem_inc(s["gate_raw"], 1)
                    dve.tensor_copy(A.V[:, :, :, 0:DH], QKV[:, :, QW + DK:].rearrange("p c (h d) -> p c h d", d=DH))
                    for src, dst, n in ((QKV[:, :, 0:QW], Of[:, :, :], NH), (QKV[:, :, QW:QW + DK], Ow[:, :, 0:DK], KV)):
                        x1, x2 = (src.rearrange("p c (h j f) -> p f c h j", j=4, f=2)[:, f] for f in range(2))
                        o1, o2 = (dst.rearrange("p c (h j f) -> p f c h j", j=4, f=2)[:, f] for f in range(2))
                        co, si = (cs[:, :, f, :].rearrange("p c (o j) -> p c o j", o=1)
                                  .broadcast_to([P, NT, n, DH // 2]) for f in range(2))
                        t0, t1 = (tmp[:, f, :, 0:n, :] for f in range(2))
                        dve.tensor_tensor(o1, x1, co, ALU.mult)
                        dve.tensor_tensor(t0, x2, si, ALU.mult).then_inc(A.s["own_dve"], 1)
                        dve.wait_ge(A.s["own_dve"], own.next())
                        dve.tensor_tensor(o1, o1, t0, ALU.subtract).then_inc(A.s["own_dve"], 1)
                        dve.wait_ge(A.s["own_dve"], own.next())
                        dve.tensor_tensor(o2, x2, co, ALU.mult)
                        dve.tensor_tensor(t1, x1, si, ALU.mult).then_inc(A.s["own_dve"], 1)
                        dve.wait_ge(A.s["own_dve"], own.next())
                        dve.tensor_tensor(o2, o2, t1, ALU.add).then_inc(A.s["own_dve"], 1)
                        dve.wait_ge(A.s["own_dve"], own.next())
                    split3(own, dve, [a[:, :, :] for a in Qp], rest, Of[:, :, :])
                    split3(own, dve, [a[:, :, :] for a in Kp], rest[:, :, 0:DK], Ow[:, :, 0:DK])
                    dve.wait_ge(s["kv_loaded"], kvl.next(16))
                    dve.tensor_copy(KBh.rearrange("j a (s d) -> j a s d", d=DH),
                                    KB.rearrange("j s (a d) -> j a s d", d=DH)).then_inc(s["kv_grouped"], 1)
                    dve.wait_ge(s["kb_ready"], kbr.next())
                    for v in range(2):
                        ins = dve.tensor_tensor(kbT[:, v, :].rearrange("p (h j) -> p h j", j=NB),
                                                ps[v].f32[:, :].rearrange("p (h j) -> p h j", j=NB),
                                                pos[:, v, :].rearrange("p (h o) -> p h o", o=1).broadcast_to([P, KV, NB]),
                                                ALU.add)
                    ins.then_inc(s["kb_taken"], 1)
                    dve.wait_ge(s["ck_ready"], ckr.next())
                    for h in range(KV):
                        dve.scalar_tensor_tensor(
                            out=CK[:, h, :, 0:NB],
                            in0=ps[0].f32[:, h * NB:(h + 1) * NB].rearrange("p (o j) -> p o j", o=1).broadcast_to([P, G, NB]),
                            scalar=b2k[:, 0:1],
                            in1=fm[:, (h % 4) * G:(h % 4 + 1) * G].rearrange("p (g o) -> p g o", o=1).broadcast_to([P, G, NB]),
                            op0=ALU.add, op1=ALU.mult)
                    dve.tensor_tensor(CV[0:NB, :, :], ps[1].f32[0:NB, 0:DK].rearrange("p (h d) -> p h d", d=DH),
                                      b2v[:, :].rearrange("p (o d) -> p o d", o=1).broadcast_to([NB, KV, DH]), ALU.add)\
                       .then_inc(s["ck_taken"], 1)
                    with loop(dve, KV, (csr, 8), (cstk, 8), (cexp, 1), (iexp, 1), (ocr, 1), (own, 16)) as kv:
                        dve.memset(imp[:, :, NB:NJ], -4000.0).then_inc(A.s["own_dve"], 1)
                        dve.wait_ge(A.s["own_dve"], own.next())
                        for c in range(NT):
                            dve.wait_ge(s["cs_ready"], csr.next())
                            dve.tensor_tensor(CS[:, c * G:(c + 1) * G, :],
                                              ps[c % 2].f32[:, 0:G * NJ].rearrange("p (g j) -> p g j", g=G),
                                              cadd[:, c:c + 1, :].broadcast_to([P, G, NJ]), ALU.add)\
                               .then_inc(s["cs_taken"], 1)
                        dve.wait_ge(s["cs_taken"], cstk.next(8))
                        dve.tensor_reduce(cmx[:, :, :], CS, AX, ALU.max).then_inc(A.s["own_dve"], 1)
                        dve.wait_ge(A.s["own_dve"], own.next())
                        dve.tensor_tensor(PC, CS, cmx[:, :, :].broadcast_to([P, NT * G, NJ]), ALU.subtract)\
                           .then_inc(s["c_sub"], 1)
                        dve.tensor_reduce(imp[:, :, 0:NB],
                                          CS.rearrange("p (c g) j -> p c j g", g=G)[:, :, 0:NB, :], AX, ALU.add)\
                           .then_inc(A.s["own_dve"], 1)
                        dve.wait_ge(A.s["own_dve"], own.next())
                        dve.tensor_reduce(m2[:, :, :], imp[:, :, :], AX, ALU.max).then_inc(A.s["own_dve"], 1)
                        dve.wait_ge(A.s["own_dve"], own.next())
                        dve.tensor_tensor(imp[:, :, :], imp[:, :, :], m2[:, :, :].broadcast_to([P, NT, NJ]), ALU.subtract)\
                           .then_inc(s["i_sub"], 1)
                        dve.wait_ge(s["c_exp"], cexp.next())
                        dve.tensor_reduce(rc[:, :, :], PC, AX, ALU.add).then_inc(A.s["own_dve"], 1)
                        dve.wait_ge(A.s["own_dve"], own.next())
                        dve.reciprocal(rc[:, :, :], rc[:, :, :]).then_inc(A.s["own_dve"], 1)
                        dve.wait_ge(A.s["own_dve"], own.next())
                        dve.wait_ge(s["i_exp"], iexp.next())
                        dve.tensor_reduce(ri[:, :, :], imp[:, :, :], AX, ALU.add).then_inc(A.s["own_dve"], 1)
                        dve.wait_ge(A.s["own_dve"], own.next())
                        dve.reciprocal(ri[:, :, :], ri[:, :, :]).then_inc(A.s["own_dve"], 1)
                        dve.wait_ge(A.s["own_dve"], own.next())
                        dve.tensor_tensor(val[:, :, :], imp[:, :, 0:NB], ri[:, :, :].broadcast_to([P, NT, NB]),
                                          ALU.mult).then_inc(A.s["own_dve"], 1)
                        dve.wait_ge(A.s["own_dve"], own.next())
                        dve.sem_inc(apart, 1)
                        for c in range(NT):
                            ins = dve.max(top[:, c, :], val[:, c, :])
                        ins.then_inc(A.s["own_dve"], 1)
                        dve.wait_ge(A.s["own_dve"], own.next())
                        dve.sem_inc(apart, 1)
                        for c in range(NT):
                            ins = dve.match_replace(mr[:, c, :], top[:, c, :], val[:, c, :], -1.0)
                        ins.then_inc(A.s["own_dve"], 1)
                        dve.wait_ge(A.s["own_dve"], own.next())
                        dve.tensor_scalar(mr[:, :, :], mr[:, :, :], 0.0, None, ALU.is_lt).then_inc(A.s["own_dve"], 1)
                        dve.wait_ge(A.s["own_dve"], own.next())
                        dve.tensor_scalar(val[:, :, :], val[:, :, :], 1e-10, None, ALU.is_gt)\
                           .then_inc(A.s["own_dve"], 1)
                        dve.wait_ge(A.s["own_dve"], own.next())
                        dve.tensor_tensor(val[:, :, :], val[:, :, :], mr[:, :, :], ALU.mult)\
                           .then_inc(A.s["own_dve"], 1)
                        dve.wait_ge(A.s["own_dve"], own.next())
                        dve.tensor_tensor(val[:, :, :], val[:, :, :], ownb[:, :, :], ALU.max)\
                           .then_inc(A.s["own_dve"], 1)
                        dve.wait_ge(A.s["own_dve"], own.next())
                        dve.tensor_scalar(MS[:, :, bass.ds(kv, 1), :].rearrange("p c o j -> p c (o j)"),
                                          val[:, :, :], -1.0, -FAR, ALU.add, ALU.mult).then_inc(A.s["own_dve"], 1)
                        dve.wait_ge(A.s["own_dve"], own.next())
                        dve.wait_ge(s["oc_ready"], ocr.next())
                        dve.tensor_tensor(Oc[:, :, bass.ds(kv * G * DH, G * DH)].rearrange("p c (g d) -> p c g d", g=G),
                                          ps[4].f32[:, 0:NT * G * DH].rearrange("p (c g d) -> p c g d", c=NT, g=G),
                                          rc[:, :, :].rearrange("p (c g) o -> p c g o", g=G).broadcast_to([P, NT, G, DH]),
                                          ALU.mult).then_inc(s["oc_taken"], 1)
                    dve.sem_inc(s["split"], 1)
                    A.dve_turn(0)
                    A.dve_turn(1)
                    A.dve_maxima()
                    A.dve_maxT()

                    def group(kv, last):
                        for g in range(G):
                            if not (last and g == G - 1):
                                A.dve_maxima()
                                A.dve_maxT()
                            if not (last and g >= G - 2):
                                A.dve_turn(g % 2)
                            A.dve_output(lambda n: (Of, Ow)[n][:, :, bass.ds(kv * G * DH + g * DH, DH)])

                    with loop(dve, KV - 1, (dc["S_ready"], NPIECE * G), (dc["S_taken"], NPIECE * G),
                              (dc["maxT_ready"], G), (dc["K_turned"], G), (dc["out_turned"], G), (own, A.OWN_HEAD * G)) as kv:
                        group(kv, False)
                    group(KV - 1, True)
                    dve.wait_ge(s["gate_ready"], gr.next())
                    dve.wait_ge(A.s["PV_taken"], (b + 1) * NH + 1)
                    hv = [o[:, :, :].rearrange("p c (h d) -> p c h d", d=DH) for o in (Oc, Of, Ow)]
                    for n in range(3):
                        ins = dve.tensor_tensor(hv[n], hv[n], GT[:, :, :, n:n + 1].broadcast_to([P, NT, NH, DH]), ALU.mult)
                    ins.then_inc(A.s["own_dve"], 1)
                    dve.wait_ge(A.s["own_dve"], own.next())
                    dve.tensor_tensor(Oc[:, :, :], Oc[:, :, :], Of[:, :, :], ALU.add).then_inc(A.s["own_dve"], 1)
                    dve.wait_ge(A.s["own_dve"], own.next())
                    dve.tensor_tensor(Oc[:, :, :], Oc[:, :, :], Ow[:, :, :], ALU.add).then_inc(s["mixed"], 1)
                    for c in range(NT):
                        if c % 2 == 0:
                            dve.wait_ge(s["out_ready"], outr.next())
                        ins = dve.tensor_tensor(xin[:, c, :], ps[4 + c // 2].f32[:, (c % 2) * D:(c % 2 + 1) * D],
                                                xin[:, c, :], ALU.add)
                        if c % 2 and c < NT - 1:
                            ins.then_inc(s["out_taken"], 1)
                    ins.then_inc(A.s["own_dve"], 1)
                    dve.wait_ge(A.s["own_dve"], own.next())
                    dve.sem_inc(s["out_taken"], 1)
                    for c in range(NT):
                        ins = dve.bn_stats(stats[:, c, :], xin[:, c, :])
                    ins.then_inc(A.s["own_dve"], 1)
                    dve.wait_ge(A.s["own_dve"], own.next())
                    dve.sem_inc(apart, 1)
                    for c in range(NT):
                        ins = dve.bn_aggr(mv[:, c, :], stats[:, c, :])
                    ins.then_inc(s["var"], 1)
                    dve.wait_ge(s["std"], std.next())
                    dve.reciprocal(rl[:, :, :], rl[:, :, :]).then_inc(A.s["own_dve"], 1)
                    dve.wait_ge(A.s["own_dve"], own.next())
                    dve.tensor_tensor(xin[:, :, :], xin[:, :, :], mv[:, :, 0:1].broadcast_to([P, NT, D]),
                                      ALU.subtract).then_inc(A.s["own_dve"], 1)
                    dve.wait_ge(A.s["own_dve"], own.next())
                    dve.tensor_tensor(xin[:, :, :], xin[:, :, :], rl[:, :, :].broadcast_to([P, NT, D]), ALU.mult)\
                       .then_inc(s["res"], 1)


def mla_stage(nc, x_in, h_out, r_out, w):
    NH, HD, RD, LAT = 16, 16, 8, 64
    with ExitStack() as ctx:
        def sb(name, shape, dt=F32):
            return ctx.enter_context(nc.sbuf_tensor("a_" + name, shape, dt))

        xin = sb("xin", [P, NT, D])
        xn = sb("xn", [P, NT, D])
        xnT = sb("xnT", [P, KD, T])
        KQ = sb("KQ", [P, T])
        Q = sb("Q", [P, NT, NH, HD])
        K = sb("K", [P, NT, NH, HD])
        Qp = [sb(f"Qp{i}", [P, NT, D], BF16) for i in range(3)]
        Kp = [sb(f"Kp{i}", [P, NT, D], BF16) for i in range(3)]
        O = sb("O", [P, NT, D])
        OT = xnT
        tmp = sb("tmp", [P, 2, NT, NH, RD // 2])
        cs = sb("cs", [P, NT, 2, RD // 2])
        Wd = sb("Wd", [P, KD, 2 * LAT])
        Wkv = sb("Wkv", [P, P + D])
        Wr = sb("Wr", [P, KD, P])
        Wo = sb("Wo", [P, KD, D])
        lnw = sb("lnw", [P, D])
        ss = sb("ss", [P, NT, 1])
        rs = sb("rs", [P, NT, 1])
        eps = sb("eps", [P, 1])
        ident = sb("ident", [P, P], BF16)
        identf = sb("identf", [P, P])
        ones = sb("ones", [2 * NT, P], BF16)
        rowmask = [sb("rowmask", [2 * NT, NT, P], BF16)]
        mask = sb("mask", [P, 7, P], BF16)
        ps = [Bank(ctx.enter_context(nc.psum_tensor(f"a_ps{i}", [P, 512], F32))) for i in range(8)]
        A = Attention(nc, ctx, "a_", 96, 96, HD, False,
                      dict(ident=ident, identf=identf, ones=ones, rowmask=[m[:, :, :] for m in rowmask], mask=mask, ps=ps, heads=NH))
        names = ("const cdma x_loaded sum root normed transposed xT_copied lat_ready lat_copied tok_ready tok_taken "
                 "split OT_ready OT_copied out_ready out_taken h_ready r_ready stored_h stored_r ones_set").split()
        s = stage_semaphores(nc, ctx, "a_", names)
        apart = A.s["apart"]
        x_v = x_in.rearrange("(b c p) d -> b p c d", p=P, c=NT)
        h_v = h_out.rearrange("(b c p) d -> b p c d", p=P, c=NT)
        r_v = r_out.rearrange("(b c p) d -> b p c d", p=P, c=NT)
        NPIECE = len(causal_probs())

        def cur(eng, *which):
            return [Cursor(eng, s[n]) for n in which]

        with nc.Block() as block:

            @block.sync
            def _(sp):
                loads = [(Wd[:, :, 0:LAT], w["kv_d_w"].rearrange("(k p) n -> p k n", p=P)),
                         (Wd[:, :, LAT:], w["q_d_w"].rearrange("(k p) n -> p k n", p=P)),
                         (Wkv[0:LAT, 0:P], w["k_u_w"]), (Wkv[0:LAT, P:], w["v_u_w"]),
                         (Wkv[LAT:, 0:P], w["q_u_w"]), (Wkv[LAT:, P:2 * P], w["rope_q_w"]),
                         (Wr[:, :, :], w["rope_k_w"].rearrange("(k p) n -> p k n", p=P)),
                         (Wo[:, :, :], w["o_w"].rearrange("(k p) n -> p k n", p=P)),
                         (lnw[:, :], w["ln1_w"].partition_broadcast(P)),
                         (cs[:, :, :, :], w["rope_cs"])]
                for dst, src in loads:
                    sp.dma_start(dst, src).then_inc(s["cdma"], 16)
                hr, rr, sh, sr = cur(sp, "h_ready", "r_ready", "stored_h", "stored_r")
                with loop(sp, BATCH, (hr, 1), (rr, 1), (sh, 16), (sr, 16)) as b:
                    sp.dma_start(xin[:, :, :], x_v[b]).then_inc(s["x_loaded"], 16)
                    sp.wait_ge(s["h_ready"], hr.next())
                    sp.dma_start(h_v[b], xn[:, :, :]).then_inc(s["stored_h"], 16)
                    sp.wait_ge(s["r_ready"], rr.next())
                    sp.dma_start(r_v[b], xin[:, :, :]).then_inc(s["stored_r"], 16)
                    sp.wait_ge(s["stored_h"], sh.next(16))
                    sp.wait_ge(s["stored_r"], sr.next(16))
                    sp.sem_inc(apart, 1)

            @block.gpsimd
            def _(pool):
                own = Cursor(pool, A.s["own_pool"])
                attention_constants(pool, own, ident, identf, ones, rowmask, mask, 1)
                pool.memset(eps[:, :], 1e-5).then_inc(A.s["own_pool"], 1)
                pool.wait_ge(A.s["own_pool"], own.next())
                pool.memset(A.mp[:, :, :, :], -3e38).then_inc(A.s["own_pool"], 1)
                pool.wait_ge(A.s["own_pool"], own.next())
                pool.memset(A.V[:, :, :, HD:], 1.0).then_inc(A.s["own_pool"], 1)
                pool.wait_ge(A.s["own_pool"], own.next())
                pool.sem_inc(s["const"], 1)
                split, tc = cur(pool, "split")[0], Cursor(pool, A.s["K_turned"])

                def stage(h, q):
                    def part(x):
                        return x[:, :, bass.ds(h * HD, HD)].rearrange("p c (o d) -> p c o d", o=1)

                    qs = A.qst[q][:, :, 0:96].rearrange("p c (a d) -> p c a d", d=HD)
                    ks = A.kst[q][:, :, 0:96].rearrange("p c (a d) -> p c a d", d=HD)
                    for a in range(3):
                        pool.tensor_copy(qs[:, :, a:a + 1, :], part(Qp[a]))
                    for a in range(2):
                        pool.tensor_copy(qs[:, :, 3 + a:4 + a, :], part(Qp[a]))
                    pool.tensor_copy(qs[:, :, 5:6, :], part(Qp[0]))
                    pool.tensor_copy(ks[:, :, 0:3, :], part(Kp[0]).broadcast_to([P, NT, 3, HD]))
                    pool.tensor_copy(ks[:, :, 3:5, :], part(Kp[1]).broadcast_to([P, NT, 2, HD]))
                    pool.tensor_copy(ks[:, :, 5:6, :], part(Kp[2])).then_inc(A.s["staged"], 1)

                with loop(pool, BATCH, (split, 1), (tc, NH)) as b:
                    pool.wait_ge(s["split"], split.next())
                    pool.sem_inc(apart, 1)
                    stage(0, 0)
                    stage(1, 1)

                    def two_heads(h0, last):
                        for q in range(2):
                            pool.wait_ge(A.s["K_turned"], tc.next())
                            pool.sem_inc(apart, 1)
                            if not last:
                                stage(h0 + q + 2, q)

                    with loop(pool, NH // 2 - 1, (tc, 2)) as h2:
                        two_heads(h2 * 2, False)
                    two_heads(NH - 2, True)

            @block.tensor
            def _(pe):
                A.pe_cursors(pe)
                xl, nrm, trc, latc, tokt, OTc, outt = cur(pe, "x_loaded", "normed", "xT_copied", "lat_copied",
                                                          "tok_taken", "OT_copied", "out_taken")
                pe.wait_ge(s["const"], 1)
                pe.wait_ge(s["cdma"], 10 * 16)
                pc = A.pc
                with loop(pe, BATCH, (nrm, 1), (trc, 4), (latc, 2), (tokt, 8), (OTc, 4), (outt, 4),
                          (pc["staged"], NH), (pc["Q_copied"], NH), (pc["K_copied"], NH), (pc["max_split"], NH),
                          (pc["Mt_ready"], NH), (pc["S_taken"], NPIECE * NH), (pc["P_ready"], NPIECE * NH),
                          (pc["PV_taken"], NH), (pc["PV_copied"], NH)) as b:
                    pe.wait_ge(s["normed"], nrm.next())
                    for j in range(4):
                        k, h = j // 2, j % 2
                        for c in range(4):
                            mm = pe.transpose(ps[j].f32[:, c * P:(c + 1) * P], xn[:, h * 4 + c, k * P:(k + 1) * P],
                                              identf[:, :])
                        mm.then_inc(s["transposed"], 1)
                    pe.wait_ge(s["xT_copied"], trc.next(4))
                    for h in range(2):
                        for k in range(KD):
                            mm = pe.matmul(ps[h].f32[:, :], Wd[:, k, :], xnT[:, k, h * 512:(h + 1) * 512],
                                           start=(k == 0), stop=(k == KD - 1))
                        mm.then_inc(s["lat_ready"], 1)
                    pe.wait_ge(s["lat_copied"], latc.next(2))
                    for c in range(NT):
                        o = 3 * (c % 2)
                        if c >= 2:
                            pe.wait_ge(s["tok_taken"], tokt.next())
                        r = slice(c * P, (c + 1) * P)
                        pe.matmul(ps[o + 0].f32[:, 0:P + D], KQ[0:LAT, r], Wkv[0:LAT, :], start=True, stop=True)
                        pe.matmul(ps[o + 1].f32[:, 0:2 * P], KQ[LAT:, r], Wkv[LAT:, 0:2 * P], start=True, stop=True)
                        for k in range(KD):
                            mm = pe.matmul(ps[o + 2].f32[:, 0:P], xnT[:, k, r], Wr[:, k, :],
                                           start=(k == 0), stop=(k == KD - 1))
                        mm.then_inc(s["tok_ready"], 1)
                    pe.wait_ge(s["tok_taken"], tokt.next(2))
                    A.pe_turn(0)
                    A.pe_turn(1)
                    A.pe_scores(0, b * NH + 2)
                    A.pe_maxT()

                    def two_heads(h0, last):
                        for q in range(2):
                            more = not (last and q)
                            A.pe_head(q, more, b * NH + h0 + q + 3, (b * NH + h0 + q + 1) * NPIECE + 2)
                            if not last:
                                A.pe_turn(q)
                            A.pe_output()

                    with loop(pe, NH // 2 - 1, (pc["staged"], 2), (pc["Q_copied"], 2), (pc["K_copied"], 2), (pc["max_split"], 2),
                              (pc["Mt_ready"], 2), (pc["S_taken"], NPIECE * 2), (pc["P_ready"], NPIECE * 2),
                              (pc["PV_taken"], 2), (pc["PV_copied"], 2)) as h2:
                        two_heads(h2 * 2, False)
                    two_heads(NH - 2, True)
                    pe.wait_ge(A.s["PV_taken"], (b + 1) * NH + 1)
                    for j in range(4):
                        k, h = j // 2, j % 2
                        for c in range(4):
                            mm = pe.transpose(ps[j].f32[:, c * P:(c + 1) * P], O[:, h * 4 + c, k * P:(k + 1) * P],
                                              identf[:, :])
                        mm.then_inc(s["OT_ready"], 1)
                    pe.wait_ge(s["OT_copied"], OTc.next(4))
                    for c in range(NT):
                        for k in range(KD):
                            mm = pe.matmul(ps[4 + c // 2].f32[:, (c % 2) * D:(c % 2 + 1) * D],
                                           OT[:, k, c * P:(c + 1) * P], Wo[:, k, :], start=(k == 0), stop=(k == KD - 1))
                        if c % 2:
                            mm.then_inc(s["out_ready"], 1)
                    pe.wait_ge(s["out_taken"], outt.next(4))

            @block.scalar
            def _(act):
                A.act_cursors(act)
                ac = A.ac
                sm, tr, latr, OTr = cur(act, "sum", "transposed", "lat_ready", "OT_ready")
                act.wait_ge(s["const"], 1)
                with loop(act, BATCH, (sm, 1), (tr, 4), (latr, 2), (OTr, 4), (ac["Q_turned"], NH),
                          (ac["ST_ready"], NPIECE * NH), (ac["PV_ready"], NH)) as b:
                    act.wait_ge(s["sum"], sm.next())
                    act.activation(rs[:, :, :], ss[:, :, :], ACT.Sqrt, bias=eps[:, 0:1], scale=1.0 / D)\
                       .then_inc(s["root"], 1)
                    for j in range(4):
                        k, h = j // 2, j % 2
                        act.wait_ge(s["transposed"], tr.next())
                        act.copy(xnT[:, k, h * 512:(h + 1) * 512], ps[j].f32[:, :]).then_inc(s["xT_copied"], 1)
                    for h in range(2):
                        act.wait_ge(s["lat_ready"], latr.next())
                        act.copy(KQ[:, h * 512:(h + 1) * 512], ps[h].f32[:, :]).then_inc(s["lat_copied"], 1)
                    A.act_turn(0, A.V[:, :, 0:1, :])
                    A.act_turn(1, A.V[:, :, 1:2, :])

                    def two_heads(h0, last):
                        for q in range(2):
                            A.act_exps()
                            A.act_output()
                            if not last:
                                A.act_turn(q, A.V[:, :, bass.ds(h0 + q + 2, 1), :])

                    with loop(act, NH // 2 - 1, (ac["Q_turned"], 2), (ac["ST_ready"], NPIECE * 2), (ac["PV_ready"], 2)) as h2:
                        two_heads(h2 * 2, False)
                    two_heads(NH - 2, True)
                    for j in range(4):
                        k, h = j // 2, j % 2
                        act.wait_ge(s["OT_ready"], OTr.next())
                        act.copy(OT[:, k, h * 512:(h + 1) * 512], ps[j].f32[:, :]).then_inc(s["OT_copied"], 1)

            @block.vector
            def _(dve):
                A.dve_cursors(dve)
                dc, own = A.dc, A.own
                xl, root, tokr, outr = cur(dve, "x_loaded", "root", "tok_ready", "out_ready")
                dve.wait_ge(s["const"], 1)
                dve.wait_ge(s["cdma"], 10 * 16)
                with loop(dve, BATCH, (xl, 16), (root, 1), (tokr, 8), (outr, 4), (dc["S_ready"], NPIECE * NH),
                          (dc["S_taken"], NPIECE * NH), (dc["maxT_ready"], NH), (dc["K_turned"], NH), (dc["out_turned"], NH),
                          (own, A.OWN_HEAD * NH + 26)) as b:
                    dve.wait_ge(s["x_loaded"], xl.next(16))
                    dve.tensor_tensor(O[:, :, :], xin[:, :, :], xin[:, :, :], ALU.mult).then_inc(A.s["own_dve"], 1)
                    dve.wait_ge(A.s["own_dve"], own.next())
                    dve.tensor_reduce(ss[:, :, :], O[:, :, :], AX, ALU.add).then_inc(s["sum"], 1)
                    dve.wait_ge(s["root"], root.next())
                    dve.reciprocal(rs[:, :, :], rs[:, :, :]).then_inc(A.s["own_dve"], 1)
                    dve.wait_ge(A.s["own_dve"], own.next())
                    dve.tensor_tensor(xn[:, :, :], xin[:, :, :], rs[:, :, :].broadcast_to([P, NT, D]), ALU.mult)\
                       .then_inc(A.s["own_dve"], 1)
                    dve.wait_ge(A.s["own_dve"], own.next())
                    dve.tensor_tensor(xn[:, :, :], xn[:, :, :], lnw[:, :].rearrange("p (o d) -> p o d", o=1)
                                      .broadcast_to([P, NT, D]), ALU.mult).then_inc(s["normed"], 1)
                    for c in range(NT):
                        o = 3 * (c % 2)
                        dve.wait_ge(s["tok_ready"], tokr.next())

                        def heads(bank, lo, n):
                            return bank.f32[:, lo:lo + NH * n].rearrange("p (h d) -> p h d", d=n)

                        dve.tensor_copy(K[:, c, :, 0:RD], heads(ps[o], 0, RD))
                        dve.tensor_copy(A.V[:, c, :, 0:HD], heads(ps[o], P, HD))
                        dve.tensor_copy(Q[:, c, :, 0:RD], heads(ps[o + 1], 0, RD))
                        dve.tensor_copy(Q[:, c, :, RD:HD], heads(ps[o + 1], P, RD))
                        ins = dve.tensor_copy(K[:, c, :, RD:HD], heads(ps[o + 2], 0, RD))
                        if c < NT - 1:
                            ins.then_inc(s["tok_taken"], 1)
                        else:
                            ins.then_inc(A.s["own_dve"], 1)
                            dve.wait_ge(A.s["own_dve"], own.next())
                            dve.sem_inc(s["tok_taken"], 1)
                    for X in (Q, K):
                        x1, x2 = X[:, :, :, RD:RD + 4], X[:, :, :, RD + 4:HD]
                        co, si = (cs[:, :, n, :].rearrange("p c (o j) -> p c o j", o=1)
                                  .broadcast_to([P, NT, NH, RD // 2]) for n in range(2))
                        dve.tensor_tensor(tmp[:, 0, :, :, :], x1, si, ALU.mult)
                        dve.tensor_tensor(tmp[:, 1, :, :, :], x2, si, ALU.mult).then_inc(A.s["own_dve"], 1)
                        dve.wait_ge(A.s["own_dve"], own.next())
                        dve.tensor_tensor(x1, x1, co, ALU.mult).then_inc(A.s["own_dve"], 1)
                        dve.wait_ge(A.s["own_dve"], own.next())
                        dve.tensor_tensor(x2, x2, co, ALU.mult).then_inc(A.s["own_dve"], 1)
                        dve.wait_ge(A.s["own_dve"], own.next())
                        dve.tensor_tensor(x1, x1, tmp[:, 1, :, :, :], ALU.subtract).then_inc(A.s["own_dve"], 1)
                        dve.wait_ge(A.s["own_dve"], own.next())
                        dve.tensor_tensor(x2, x2, tmp[:, 0, :, :, :], ALU.add).then_inc(A.s["own_dve"], 1)
                        dve.wait_ge(A.s["own_dve"], own.next())
                    dve.tensor_scalar(Q[:, :, :, :], Q[:, :, :, :], float(HD) ** -0.5, None, ALU.mult)\
                       .then_inc(A.s["own_dve"], 1)
                    dve.wait_ge(A.s["own_dve"], own.next())
                    for X, parts in ((Q, Qp), (K, Kp)):
                        split3(own, dve, [a[:, :, :] for a in parts], O[:, :, :],
                               X[:, :, :, :].rearrange("p c h d -> p c (h d)"))
                    dve.sem_inc(s["split"], 1)
                    A.dve_turn(0)
                    A.dve_turn(1)
                    A.dve_maxima()
                    A.dve_maxT()

                    def two_heads(h0, last):
                        for q in range(2):
                            if not (last and q):
                                A.dve_maxima()
                                A.dve_maxT()
                            if not last:
                                A.dve_turn(q)
                            A.dve_output(lambda n: O[:, :, bass.ds((h0 + q) * HD, HD)])

                    with loop(dve, NH // 2 - 1, (dc["S_ready"], NPIECE * 2), (dc["S_taken"], NPIECE * 2),
                              (dc["maxT_ready"], 2), (dc["K_turned"], 2), (dc["out_turned"], 2), (own, A.OWN_HEAD * 2)) as h2:
                        two_heads(h2 * 2, False)
                    two_heads(NH - 2, True)
                    for c in range(NT):
                        if c % 2 == 0:
                            dve.wait_ge(s["out_ready"], outr.next())
                        ins = dve.tensor_tensor(xn[:, c, :], ps[4 + c // 2].f32[:, (c % 2) * D:(c % 2 + 1) * D],
                                                xin[:, c, :], ALU.add)
                        if c % 2 and c < NT - 1:
                            ins.then_inc(s["out_taken"], 1)
                    ins.then_inc(A.s["own_dve"], 1)
                    dve.wait_ge(A.s["own_dve"], own.next())
                    dve.sem_inc(s["out_taken"], 1)
                    dve.sem_inc(s["h_ready"], 1)
                    dve.tensor_tensor(xin[:, :, :], xin[:, :, :], xn[:, :, :], ALU.add).then_inc(s["r_ready"], 1)


def build_program(nc, t):
    def scratch(name, shape):
        return nc.dram_tensor(name, shape, F32, kind="Internal").ap()

    x1, x2, x3, h, r = (scratch(n, (BATCH * T, D)) for n in ("x1_rows", "x2_rows", "x3_rows", "h_rows", "r_rows"))
    kv_rows = scratch("kv_rows", (T, 2 * 64))
    ssd_stage(nc, t["x"], x1, {k[2:]: v for k, v in t.items() if k.startswith("s_")})
    moe_stage(nc, x1, x1, x2, t["m_router"], t["m_gate_up"].rearrange("e (k p) n -> e p k n", p=P), t["m_down"],
              lora={k: t["m_" + k] for k in ("rA", "rBT", "gA", "gB", "dA", "dB")})
    nsa_stage(nc, x2, x3, kv_rows, {k[2:]: v for k, v in t.items() if k.startswith("n_")})
    mla_stage(nc, x3, h, r, {k[2:]: v for k, v in t.items() if k.startswith("a_")})
    moe_stage(nc, h, r, t["out"], t["e_router"], t["e_gate_up"].rearrange("e (k p) n -> e p k n", p=P), t["e_down"],
              rms_w=t["e_ln_w"], router_b=t["e_router_b"])




def rope_table():
    inv = (1.0 / 10000.0 ** (np.arange(0, 8, 2, dtype=np.float32) / 8)).astype(np.float32)
    ang = np.outer(np.arange(T, dtype=np.float32), inv).astype(np.float32)
    table = np.stack([np.cos(ang), np.sin(ang)], 1).astype(np.float32)
    return table.reshape(NT, P, 2, 4).transpose(1, 0, 2, 3)


def pair_rows(a):
    v = a.reshape(32, 2, 32, 2)
    return [x.transpose(1, 3, 2, 0).reshape(P, 32) for x in (v, v[..., ::-1])]


def laid_out(i):
    def first(prefix, names):
        return {k: i[prefix + k] for k in names.split()}

    s, m, n, e = "L0_attn_", "L0_ffn_", "L1_attn_", "L1_ffn_"
    t = {"x": i[s + "x"].reshape(BATCH * T, D)}
    t |= {"s_" + k: v for k, v in {
        "W_in": i[s + "W_in"], "W_out": i[s + "W_out"], "norm_w": i[s + "norm_w"].reshape(4, P).T,
        "freq": i[s + "rope_freqs"], "dt_bias": i[s + "dt_bias"].reshape(64, 1), "A_log": i[s + "A_log"].reshape(64, 1),
        "D_param": i[s + "D_param"],
        "bias": np.stack(pair_rows(i[s + "B_bias"]) + pair_rows(i[s + "C_bias"]), 1)}.items()}
    t |= {"m_" + k: v for k, v in {
        "router": i[m + "gate_weight"].T, "rA": i[m + "gate_lora_A"], "rBT": i[m + "gate_lora_B"].T,
        "gate_up": i[m + "gate_up_proj"], "down": i[m + "down_proj"], "gA": i[m + "gup_lora_A"],
        "gB": i[m + "gup_lora_B"].transpose(0, 2, 1), "dA": i[m + "down_lora_A"],
        "dB": i[m + "down_lora_B"].transpose(0, 2, 1)}.items()}
    t |= {"n_" + k: v for k, v in {
        **first(n, "w_qkv w_gate w_out k_cw1 v_cw1 v_cw2 v_cb2 b_gate"),
        "cb1": np.stack([i[n + "k_cb1"], i[n + "v_cb1"]], 1), "k_cw2": np.tile(i[n + "k_cw2"], (1, 16)),
        "k_cb2": np.tile(i[n + "k_cb2"], 16).reshape(P, 1),
        "mem_ck": np.broadcast_to(i[n + "mem_ck"].reshape(2, 4, 1, 8), (2, 4, 4, 8)).reshape(2, P).T,
        "mem_cv": i[n + "mem_cv"].reshape(1, 8, 8),
        "pos": np.stack([i[n + "k_pos"].reshape(8, P).T, i[n + "v_pos"].reshape(8, P).T], 1),
        "rope_cs": rope_table()}.items()}
    t |= {"a_" + k: v for k, v in {
        **first(e, "kv_d_w q_d_w k_u_w v_u_w q_u_w rope_k_w rope_q_w o_w ln1_w"), "rope_cs": rope_table()}.items()}
    t |= {"e_" + k: v for k, v in {
        "router": i[e + "router_w"], "router_b": i[e + "router_b"], "ln_w": i[e + "ln2_w"],
        "gate_up": np.concatenate([np.concatenate([i[e + "r_gate"], i[e + "r_up"]], 2),
                                   np.concatenate([i[e + "sh_gate"], i[e + "sh_up"]], 1)[None]], 0),
        "down": np.concatenate([i[e + "r_down"], i[e + "sh_down"][None]], 0)}.items()}
    return {k: np.ascontiguousarray(v) for k, v in t.items()}


def kernel(**inputs):
    import concourse.bacc as bacc
    from concourse.bass_utils import run_bass_kernel_spmd

    nc = bacc.Bacc("TRN2", target_bir_lowering=False, num_devices=1)
    arrays = {"in_" + k: v for k, v in laid_out({k: np.asarray(v) for k, v in inputs.items()}).items()}
    tensors = {k[3:]: nc.dram_tensor(k, a.shape, mybir.dt.from_np(a.dtype), kind="ExternalInput").ap()
               for k, a in arrays.items()}
    tensors["out"] = nc.dram_tensor("out_rows", (BATCH * T, D), F32, kind="ExternalOutput").ap()
    build_program(nc, tensors)
    r = run_bass_kernel_spmd(nc, [arrays], core_ids=[0])
    return r.results[0]["out_rows"].reshape(BATCH, T, D)
```
